# Optimizing a Trainium2 kernel written in Bass

```python
import numpy as np
import jax
import jax.numpy as jnp

def _softmax(x, axis=-1):
    return jax.nn.softmax(x, axis=axis)

def _gelu(x):
    return jax.nn.gelu(x, approximate=True)

def _silu(x):
    return jax.nn.silu(x)

def _sigmoid(x):
    return jax.nn.sigmoid(x)

def _layernorm(x, axis=-1, eps=1e-05):
    m = jnp.mean(x, axis=axis, keepdims=True)
    v = jnp.var(x, axis=axis, keepdims=True)
    return (x - m) / jnp.sqrt(v + eps)

def _scatter_add(tgt, idx, src, axis=0):
    return tgt.at[idx].add(src)

def _segment_sum(src, seg, n):
    return jax.ops.segment_sum(src, seg, n)
kernel_name = 'mk_prb_d1_jaxref_r8_6bbae1'

def setup_inputs(seed: int=0):
    np.random.seed(seed)
    _w = jnp.asarray

    def _L0_attn_setup():
        import jax, jax.numpy as jnp
        import numpy as np
        B, S, E = (4, 128, 128)
        H = 16
        D = E // H
        key = jax.random.key(seed)
        kx, kq, kk, kv, ko = jax.random.split(key, 5)
        scale = 1.0 / np.sqrt(2.0 * E)
        return {'x': jax.random.normal(kx, (B, S, E), dtype=jnp.float32), 'Wq': jax.random.normal(kq, (E, E), dtype=jnp.float32) * scale, 'Wk': jax.random.normal(kk, (E, E), dtype=jnp.float32) * scale, 'Wv': jax.random.normal(kv, (E, E), dtype=jnp.float32) * scale, 'Wo': jax.random.normal(ko, (E, E), dtype=jnp.float32) * scale}
    _L0_attn_in = _L0_attn_setup()

    def _L0_ffn_setup():
        import jax, jax.numpy as jnp
        import numpy as np
        S, B, H = (256, 1, 128)
        N_HEADS = 16
        HEAD_DIM = H // N_HEADS
        E, K, F = (8, 2, 256)
        EPS = 1e-05

        def layernorm(x, w, b):
            mu = jnp.mean(x, axis=-1, keepdims=True)
            var = jnp.mean(jnp.square(x - mu), axis=-1, keepdims=True)
            return (x - mu) * jax.lax.rsqrt(var + EPS) * w + b
        key = jax.random.key(seed)
        ks = jax.random.split(key, 8)
        std = 0.02
        return {'x': jax.random.normal(ks[0], (S, B, H), dtype=jnp.float32), 'ln1_w': jnp.ones((H,), jnp.float32), 'ln1_b': jnp.zeros((H,), jnp.float32), 'in_proj_w': jax.random.normal(ks[1], (3 * H, H), jnp.float32) * std, 'in_proj_b': jnp.zeros((3 * H,), jnp.float32), 'out_proj_w': jax.random.normal(ks[2], (H, H), jnp.float32) * std, 'out_proj_b': jnp.zeros((H,), jnp.float32), 'ln2_w': jnp.ones((H,), jnp.float32), 'ln2_b': jnp.zeros((H,), jnp.float32), 'router_w': jax.random.normal(ks[3], (E, H), jnp.float32) * std, 'w1': jax.random.normal(ks[4], (E, H, F), jnp.float32) * std, 'w2': jax.random.normal(ks[5], (E, F, H), jnp.float32) * std}
    _L0_ffn_in = _L0_ffn_setup()
    _d = {'L0_attn_x': _L0_attn_in['x'], 'L0_attn_Wq': _L0_attn_in['Wq'], 'L0_attn_Wk': _L0_attn_in['Wk'], 'L0_attn_Wv': _L0_attn_in['Wv'], 'L0_attn_Wo': _L0_attn_in['Wo'], 'L0_ffn_ln1_w': _L0_ffn_in['ln1_w'], 'L0_ffn_ln1_b': _L0_ffn_in['ln1_b'], 'L0_ffn_in_proj_w': _L0_ffn_in['in_proj_w'], 'L0_ffn_in_proj_b': _L0_ffn_in['in_proj_b'], 'L0_ffn_out_proj_w': _L0_ffn_in['out_proj_w'], 'L0_ffn_out_proj_b': _L0_ffn_in['out_proj_b'], 'L0_ffn_ln2_w': _L0_ffn_in['ln2_w'], 'L0_ffn_ln2_b': _L0_ffn_in['ln2_b'], 'L0_ffn_router_w': _L0_ffn_in['router_w'], 'L0_ffn_w1': _L0_ffn_in['w1'], 'L0_ffn_w2': _L0_ffn_in['w2']}
    _x0 = _d['L0_attn_x']
    _d['L0_attn_x'] = jax.random.normal(jax.random.fold_in(jax.random.key(seed), 1), (32, 256, 128), dtype=_x0.dtype)
    del _x0
    return _d

def reference(L0_attn_x, L0_attn_Wq, L0_attn_Wk, L0_attn_Wv, L0_attn_Wo, L0_ffn_ln1_w, L0_ffn_ln1_b, L0_ffn_in_proj_w, L0_ffn_in_proj_b, L0_ffn_out_proj_w, L0_ffn_out_proj_b, L0_ffn_ln2_w, L0_ffn_ln2_b, L0_ffn_router_w, L0_ffn_w1, L0_ffn_w2):

    def _L0_attn_ref(x, Wq, Wk, Wv, Wo):
        import jax, jax.numpy as jnp
        import numpy as np
        B, S, E = (4, 128, 128)
        H = 16
        D = E // H
        b, s, e = x.shape

        def split_heads(t):
            return t.reshape(b, s, H, D).transpose(0, 2, 1, 3)
        q = split_heads(x @ Wq)
        k = split_heads(x @ Wk)
        v = split_heads(x @ Wv)
        qc = q - q.mean(axis=-1, keepdims=True)
        kc = k - k.mean(axis=-1, keepdims=True)
        cov = jnp.einsum('bhsd,bhtd->bhst', qc, kc) / D
        q_var = jnp.var(q, axis=-1, ddof=1)
        k_var = jnp.var(k, axis=-1, ddof=1)
        var_comp = q_var[..., :, None] * k_var[..., None, :] / D
        scores = cov + var_comp
        attn = jax.nn.softmax(scores, axis=-1)
        out = jnp.einsum('bhst,bhtd->bhsd', attn, v)
        out = out.transpose(0, 2, 1, 3).reshape(b, s, e)
        return out @ Wo

    def _L0_ffn_ref(x, ln1_w, ln1_b, in_proj_w, in_proj_b, out_proj_w, out_proj_b, ln2_w, ln2_b, router_w, w1, w2):
        import jax, jax.numpy as jnp
        import numpy as np
        S, B, H = (256, 1, 128)
        N_HEADS = 16
        HEAD_DIM = H // N_HEADS
        E, K, F = (8, 2, 256)
        EPS = 1e-05

        def layernorm(x, w, b):
            mu = jnp.mean(x, axis=-1, keepdims=True)
            var = jnp.mean(jnp.square(x - mu), axis=-1, keepdims=True)
            return (x - mu) * jax.lax.rsqrt(var + EPS) * w + b
        s, b, h = x.shape
        hn = layernorm(x, ln1_w, ln1_b)
        qkv = hn @ in_proj_w.T + in_proj_b
        q, k, v = jnp.split(qkv, 3, axis=-1)
        q = q.reshape(s, b, N_HEADS, HEAD_DIM)
        k = k.reshape(s, b, N_HEADS, HEAD_DIM)
        v = v.reshape(s, b, N_HEADS, HEAD_DIM)
        scores = jnp.einsum('sbnd,tbnd->bnst', q, k) / np.sqrt(HEAD_DIM)
        causal = jnp.tril(jnp.ones((s, s), bool))
        scores = jnp.where(causal[None, None], scores, -jnp.inf)
        probs = jax.nn.softmax(scores, axis=-1)
        attn = jnp.einsum('bnst,tbnd->sbnd', probs, v).reshape(s, b, h)
        attn = attn @ out_proj_w.T + out_proj_b
        x1 = x + attn
        hn2 = layernorm(x1, ln2_w, ln2_b).reshape(s * b, h)
        logits = hn2 @ router_w.T
        rp = jax.nn.softmax(logits, axis=-1)
        topw, topi = jax.lax.top_k(rp, K)
        gates = jnp.sum(jax.nn.one_hot(topi, E, dtype=hn2.dtype) * topw[..., None], axis=1)
        hmid = jax.nn.gelu(jnp.einsum('th,ehf->tef', hn2, w1), approximate=False)
        y = jnp.einsum('tef,efh->th', hmid * gates[:, :, None], w2)
        return x1 + y.reshape(s, b, h)
    x = L0_attn_x
    xn = _layernorm(x, axis=-1)
    x = x + _L0_attn_ref(xn, L0_attn_Wq, L0_attn_Wk, L0_attn_Wv, L0_attn_Wo) + _L0_ffn_ref(xn, L0_ffn_ln1_w, L0_ffn_ln1_b, L0_ffn_in_proj_w, L0_ffn_in_proj_b, L0_ffn_out_proj_w, L0_ffn_out_proj_b, L0_ffn_ln2_w, L0_ffn_ln2_b, L0_ffn_router_w, L0_ffn_w1, L0_ffn_w2)
    return x

_drawn_inputs = setup_inputs


def setup_inputs(seed=0):
    import zlib

    import numpy as np

    out = dict(_drawn_inputs(seed))
    spreads = {'L0_ffn_ln1_w': (1.0, 0.6),
     'L0_ffn_ln1_b': (0.0, 0.8),
     'L0_ffn_in_proj_b': (0.0, 0.643),
     'L0_ffn_out_proj_b': (0.0, 0.1),
     'L0_ffn_ln2_w': (1.0, 0.6),
     'L0_ffn_ln2_b': (0.0, 0.8)}
    factors = {'L0_attn_Wq': 8.0,
     'L0_attn_Wk': 8.0,
     'L0_attn_Wv': 3.477,
     'L0_attn_Wo': 3.471,
     'L0_ffn_in_proj_w': 5.426,
     'L0_ffn_out_proj_w': 3.585,
     'L0_ffn_router_w': 8.0,
     'L0_ffn_w1': 8.0,
     'L0_ffn_w2': 8.0}
    for name, (base, spread) in spreads.items():
        noise = np.random.default_rng([zlib.crc32(name.encode()), seed]).standard_normal(out[name].shape)
        drawn = base * np.exp(spread * noise) if base else spread * noise
        out[name] = jnp.asarray(drawn.astype(out[name].dtype))
    for name, factor in factors.items():
        out[name] = (out[name] * factor).astype(out[name].dtype)
    return out
```

```python
from contextlib import ExitStack

import concourse.bass as bass
from concourse import mybir

F32 = mybir.dt.float32
BF16 = mybir.dt.bfloat16
U32 = mybir.dt.uint32
ALU = mybir.AluOpType
ACT = mybir.ActivationFunctionType
AX = mybir.AxisListType

P = 128
NB, NS, E = 32, 256, 128
H = 16
D = E // H
EPS = 1e-5
ST = NS // P

FEAT = D + 1
STACK = 64
SHIFT = 2 * FEAT
SPARTS = 2
PAIRS = H // 2
HP = PAIRS // 2
SROWS = 2 * SPARTS * HP

PE_AT = dict(q1=0, k1=2, out1=5, merge=8, project=10, q0=12, out0=14,
             shift1=2, v=4, x=6, shift0=10, k0=13, qk=15)
DVE_AT = dict(q1=0, statistics=1, normalise=3, first=4, repeat1=5, out1=6, second=7,
              shift0=8, repeat2=9, output=11, q0=13, out0=15)
ACT_AT = dict(copy_out1=0, features=0, shift1=2, k1=3, v=5, x=7, merged=9, shift0=11, copy_out0=10, k0=13)

TILES = 4
QUAD = 4
SEQ = 32
GPOS = TILES * QUAD
GROUPS = NS // GPOS
TOK = TILES * P
NE, FF = 8, 256
FC = FF // P
MASKED = -1.0e30


def positive(count):
    return not isinstance(count, int) or count > 0


def present(b):
    if not isinstance(b, int):
        return (True,) * 5
    return tuple(0 <= b + d < NB for d in range(-1, 4))


def run_steps(eng, step):
    for b in range(-3, 3):
        step(b, b % 2)
    with eng.Fori(0, NB // 2 - 4) as i:
        step(2 * i + 3, 1)
        step(2 * i + 4, 0)
    for b in range(NB - 5, NB + 1):
        step(b, b % 2)


def group_present(g):
    if not isinstance(g, int):
        return (True,) * 4
    return tuple(0 <= g + d < GROUPS for d in range(4))


def run_groups(eng, step):
    for g in range(-3, 1):
        step(g, g % 2)
    with eng.Fori(0, GROUPS // 2 - 2) as i:
        step(2 * i + 1, 1)
        step(2 * i + 2, 0)
    for g in range(GROUPS - 3, GROUPS):
        step(g, g % 2)


class Own:

    def __init__(self):
        self.count = 0

    def next(self):
        self.count += 1
        return self.count


def attention_and_experts_kernel(nc, x, Wq, Wk, Wv, Wo, ln1_w, ln1_b, in_w_t, in_b, out_w_t, out_b,
                                 ln2_w, ln2_b, router_t, w1, w2, out):
    ctx = ExitStack()
    with ctx:
        def sb(name, shape, dt=F32):
            return ctx.enter_context(nc.sbuf_tensor(name, shape, dt))

        def sem(name):
            return ctx.enter_context(nc.semaphore(name))

        z_dram = nc.dram_tensor("z_scratch", (NB, NS, E), F32).ap()

        bank = [ctx.enter_context(nc.psum_tensor(f"bank{i}", [P, 512], F32)) for i in range(8)]
        row_scores = bank[0:3]
        col_scores = bank[3:5]
        pv_bank = bank[5]
        misc = bank[6:8]
        up_bank, down_bank, seq_bank = bank[0:2], bank[2:4], bank[4:6]

        ident = sb("ident", [P, P])
        identb = sb("identb", [P, P], BF16)
        wqk = sb("wqk", [P, 2, H, D])
        wqk_raw = sb("wqk_raw", [P, 2, H, D])
        wqk_mean = sb("wqk_mean", [P, 2 * H])
        wv = sb("wv", [P, E])
        wo = sb("wo", [P, E])

        x_in = [sb(f"x_in{p}", [P, ST, E]) for p in range(2)]
        stats = sb("stats", [P, ST, 6])
        mv = sb("mv", [P, ST, 2])
        rstd = sb("rstd", [P, ST])
        minus_half = sb("minus_half", [P, TILES])
        epsilon = sb("epsilon", [P, TILES])
        xn = sb("xn", [P, ST, E])
        xnT = [sb(f"xnT{p}", [P, NS]) for p in range(2)]
        feat = sb("feat", [P, 2, ST * H, FEAT])
        resid = sb("resid", [P, 2, ST * H, FEAT])
        sq = sb("sq", [P, 2, ST * H, D])
        stack = sb("stack", [P, 2, ST, H, STACK], BF16)
        flat = "p a g k -> p (a g) k"
        parts = stack[:].rearrange("p a s h k -> p (a s h) k")
        slots = stack[:, :, :, :, 0:7 * FEAT].rearrange("p a s h (m k) -> p a (s h) m k", k=FEAT)
        QT = [sb(f"QT{p}", [P, PAIRS, NS], BF16) for p in range(2)]
        KT = [[sb(f"KT{p}_{a}", [P, PAIRS, NS], BF16) for a in range(2)] for p in range(2)]
        V = [sb(f"V{p}", [P, ST, H, FEAT]) for p in range(2)]
        rowmax = [sb(f"rowmax{k}", [P, ST, 2, HP]) for k in range(2)]
        shift = [sb(f"shift{k}", [P, ST, 2, SPARTS, HP], BF16) for k in range(2)]
        shiftT = [sb(f"shiftT{k}", [SROWS, NS], BF16) for k in range(2)]
        prob = sb("prob", [P, 8, ST, NS])
        oT = [sb(f"oT{k}", [P, 2, NS]) for k in range(2)]
        rsum = [sb(f"rsum{k}", [P, 2, ST, 4]) for k in range(2)]
        o_nat = sb("o_nat", [P, ST, H, D])
        oT_all = sb("oT_all", [P, NS])
        z_out = [sb(f"z_out{p}", [P, ST, E]) for p in range(2)]

        in_wT = sb("in_wT", [P, 3 * E])
        in_bT = sb("in_bT", [P, 3])
        out_wT = sb("out_wT", [P, E])
        ob_raw = sb("ob_raw", [P, E])
        ob_row = sb("ob_row", [P, E])
        bv_wide = sb("bv_wide", [P, P])
        ln1w, ln1b, ln2w, ln2b = (sb(n, [P, 1]) for n in ("ln1w", "ln1b", "ln2w", "ln2b"))
        router = sb("router", [P, NE])
        w1_sb = sb("w1_sb", [P, NE, FF])
        w2_sb = sb("w2_sb", [P, NE, FC, E])
        head_mask = sb("head_mask", [P, H])
        head_bias = sb("head_bias", [P, H])
        seq_eye = sb("seq_eye", [SEQ, QUAD, SEQ], BF16)
        causal = sb("causal", [SEQ, H, SEQ], BF16)
        index8 = sb("index8", [P, TILES, NE])
        xg = [sb(f"xg{p}", [P, TILES, E]) for p in range(2)]
        zg = [sb(f"zg{p}", [P, TILES, E]) for p in range(2)]
        xzg = [sb(f"xzg{p}", [P, TILES, E]) for p in range(2)]
        gstats = sb("gstats", [P, TILES, 6])
        gmv = sb("gmv", [P, TILES, 2])
        gr1 = sb("gr1", [P, TILES])
        gr2 = sb("gr2", [P, TILES])
        gr12 = sb("gr12", [P, TILES])
        gt = sb("gt", [P, TILES])
        gxh = sb("gxh", [P, TILES, E])
        gxb = [sb(f"gxb{p}", [P, TILES, E]) for p in range(2)]
        hnT = sb("hnT", [P, TOK])
        gqT = sb("gqT", [P, TOK])
        Kexp = sb("Kexp", [P, GPOS, H, SEQ])
        Vexp = sb("Vexp", [P, TILES, H, QUAD, FEAT])
        smax = sb("smax", [P, TILES, H])
        sdiff = prob[:, 0:4].rearrange("p t s (h k) -> p t (s h) k", k=SEQ)
        sprob = prob[:, 4:8].rearrange("p t s (h k) -> p t (s h) k", k=SEQ)
        sprobT = sb("sprobT", [P, TILES, H, SEQ])
        srec = [sb(f"srec{k}", [P, H // 2, QUAD]) for k in range(2)]
        so_nat = sb("so_nat", [P, QUAD, H, D])
        aT = sb("aT", [P, TILES, QUAD, SEQ])
        x1 = sb("x1", [P, TILES, E])
        stats2 = sb("stats2", [P, TILES, 6])
        mv2 = sb("mv2", [P, TILES, 2])
        rstd2 = sb("rstd2", [P, TILES])
        h2n = sb("h2n", [P, TILES, E])
        hn2T = [sb(f"hn2T{p}", [P, TOK]) for p in range(2)]
        logit = sb("logit", [P, TILES, NE])
        top = sb("top", [P, TILES, 8])
        topi = sb("topi", [P, TILES, 8], U32)
        topf = sb("topf", [P, TILES, 2])
        pick = sb("pick", [P, 2, TILES, NE])
        ldiff = sb("ldiff", [P, TILES, NE])
        lexp = sb("lexp", [P, TILES, NE])
        lsum = sb("lsum", [P, TILES])
        gate = [sb(f"gate{p}", [P, TILES, NE]) for p in range(2)]
        hmid = [[sb(f"hmid{k}_{c}", [P, TOK]) for c in range(FC)] for k in range(2)]
        acc = [sb(f"acc{p}", [P, TILES, E]) for p in range(2)]

        s_dma_w = sem("s_dma_w")
        s_dma_w2 = sem("s_dma_w2")
        s_ident = sem("s_ident")
        s_pool = sem("s_pool")
        s_setup = sem("s_setup")
        s_bvw = sem("s_bvw")
        s_dve = sem("s_dve")
        s_x = [sem(f"s_x{p}") for p in range(2)]
        s_var = sem("s_var")
        s_rstd = sem("s_rstd")
        s_xn = sem("s_xn")
        s_xt_ps = sem("s_xt_ps")
        s_xt = sem("s_xt")
        s_qk_ps = sem("s_qk_ps")
        s_feat = sem("s_feat")
        s_v_ps = sem("s_v_ps")
        s_v = sem("s_v")
        s_ninth = sem("s_ninth")
        s_first = sem("s_first")
        s_resid = sem("s_resid")
        s_second = sem("s_second")
        s_third = sem("s_third")
        s_stack = sem("s_stack")
        s_qt_ps, s_qt, s_kt_ps, s_kt = ([sem(f"{n}{k}") for k in range(2)] for n in
                                        ("s_qt_ps", "s_qt", "s_kt_ps", "s_kt"))
        s_shift = [sem(f"s_shift{k}") for k in range(2)]
        s_sht_ps = [sem(f"s_sht_ps{k}") for k in range(2)]
        s_sht = [sem(f"s_sht{k}") for k in range(2)]
        s_shd = [sem(f"s_shd{k}") for k in range(2)]
        s_ot = [sem(f"s_ot{k}") for k in range(2)]
        s_on_ps = [sem(f"s_on_ps{k}") for k in range(2)]
        s_on = [sem(f"s_on{k}") for k in range(2)]
        s_row = sem("s_row")
        s_max = sem("s_max")
        s_col = sem("s_col")
        s_exp = sem("s_exp")
        s_pv = sem("s_pv")
        s_oa_ps = sem("s_oa_ps")
        s_oa = sem("s_oa")
        s_pr_ps = sem("s_pr_ps")
        s_z = sem("s_z")
        s_zd = [sem(f"s_zd{p}") for p in range(2)]

        s_xg = [sem(f"s_xg{p}") for p in range(2)]
        s_zg = [sem(f"s_zg{p}") for p in range(2)]
        s_xzg = sem("s_xzg")
        s_gvar = sem("s_gvar")
        s_gr = sem("s_gr")
        s_gxh = sem("s_gxh")
        s_gxb = sem("s_gxb")
        s_hn_ps = sem("s_hn_ps")
        s_hn = sem("s_hn")
        s_gq_ps = sem("s_gq_ps")
        s_gq = sem("s_gq")
        s_gk_ps = sem("s_gk_ps")
        s_kexp = sem("s_kexp")
        s_gv_ps = sem("s_gv_ps")
        s_vexp = sem("s_vexp")
        s_sc = sem("s_sc")
        s_sdiff = sem("s_sdiff")
        s_sprob = sem("s_sprob")
        s_spT = sem("s_spT")
        s_spv = sem("s_spv")
        s_son = sem("s_son")
        s_a_ps = sem("s_a_ps")
        s_a = sem("s_a")
        s_pj_ps = sem("s_pj_ps")
        s_xattn = sem("s_xattn")
        s_var2 = sem("s_var2")
        s_rstd2 = sem("s_rstd2")
        s_h2n = sem("s_h2n")
        s_h2_ps = sem("s_h2_ps")
        s_h2 = sem("s_h2")
        s_lg_ps = sem("s_lg_ps")
        s_ld = sem("s_ld")
        s_le = sem("s_le")
        s_gate = sem("s_gate")
        s_up = sem("s_up")
        s_mid = sem("s_mid")
        s_dn = sem("s_dn")
        s_acc = sem("s_acc")
        s_acc0 = sem("s_acc0")
        s_out = [sem(f"s_out{p}") for p in range(2)]

        block = ctx.enter_context(nc.Block())

        @block.gpsimd
        def _(pool):
            own = Own()
            for dst, src in ((wqk_raw[:, 0], Wq.rearrange("e (h d) -> e h d", h=H)),
                             (wqk_raw[:, 1], Wk.rearrange("e (h d) -> e h d", h=H)),
                             (wv[:], Wv), (wo[:], Wo)):
                pool.dma_start(dst, src).then_inc(s_dma_w, 16)
            pool.memset(minus_half[:], -0.5).then_inc(s_pool, 1)
            pool.wait_ge(s_pool, own.next())
            pool.memset(epsilon[:], EPS).then_inc(s_pool, 1)
            pool.wait_ge(s_pool, own.next())
            pool.memset(ident[:], 0.0).then_inc(s_pool, 1)
            pool.wait_ge(s_pool, own.next())
            pool.affine_select(out=ident[:], in_=ident[:], compare_op=ALU.not_equal, fill=1.0,
                               base=0, pattern=[[-1, P]], channel_multiplier=1).then_inc(s_pool, 1)
            pool.wait_ge(s_pool, own.next())
            pool.tensor_copy(identb[:], ident[:]).then_inc(s_ident, 1)
            for dst, src in ((in_wT[:], in_w_t), (in_bT[:], in_b.rearrange("(c p) -> p c", p=P)),
                             (out_wT[:], out_w_t), (ob_raw[:], out_b.rearrange("(a e) -> a e", a=1).broadcast_to([P, E])),
                             (ln1w[:], ln1_w.rearrange("(p a) -> p a", a=1)),
                             (ln1b[:], ln1_b.rearrange("(p a) -> p a", a=1)),
                             (ln2w[:], ln2_w.rearrange("(p a) -> p a", a=1)),
                             (ln2b[:], ln2_b.rearrange("(p a) -> p a", a=1)),
                             (router[:], router_t),
                             (w1_sb[:], w1.rearrange("e h f -> h e f")),
                             (w2_sb[:], w2.rearrange("e (c f) h -> f e c h", c=FC))):
                with nc.allow_non_contiguous_dma(reason="the biases, once"):
                    pool.dma_start(dst, src).then_inc(s_dma_w2, 16)
            pool.memset(head_mask[:], 1.0).then_inc(s_pool, 1)
            pool.wait_ge(s_pool, own.next())
            pool.affine_select(out=head_mask[:], in_=head_mask[:], compare_op=ALU.is_ge, fill=0.0,
                               base=0, pattern=[[-D, H]], channel_multiplier=1).then_inc(s_pool, 1)
            pool.wait_ge(s_pool, own.next())
            pool.affine_select(out=head_mask[:], in_=head_mask[:], compare_op=ALU.is_ge, fill=0.0,
                               base=D - 1, pattern=[[D, H]], channel_multiplier=-1).then_inc(s_pool, 1)
            pool.wait_ge(s_pool, own.next())
            pool.memset(seq_eye[:], 0.0).then_inc(s_pool, 1)
            pool.wait_ge(s_pool, own.next())
            pool.affine_select(out=seq_eye[:], in_=seq_eye[:], compare_op=ALU.not_equal, fill=1.0,
                               base=0, pattern=[[0, QUAD], [-1, SEQ]], channel_multiplier=1).then_inc(s_pool, 1)
            pool.wait_ge(s_pool, own.next())
            pool.memset(causal[:], 0.0).then_inc(s_pool, 1)
            pool.wait_ge(s_pool, own.next())
            pool.affine_select(out=causal[:], in_=causal[:], compare_op=ALU.is_ge, fill=MASKED,
                               base=0, pattern=[[0, H], [-1, SEQ]], channel_multiplier=1).then_inc(s_pool, 1)
            pool.wait_ge(s_pool, own.next())
            for e in range(NE):
                ins = pool.memset(index8[:, :, e:e + 1], float(e))
            ins.then_inc(s_ident, 1)

            def deviation(n):
                pool.wait_ge(s_var, n + 1)
                pool.tensor_tensor(rstd[:], mv[:, :, 1], epsilon[:, 0:ST], ALU.add).then_inc(s_pool, 1)
                pool.wait_ge(s_pool, own.next())
                pool.tensor_tensor(rstd[:], rstd[:], minus_half[:, 0:ST], ALU.pow).then_inc(s_rstd, 1)

            def variance(n):
                pool.wait_ge(s_feat, 2 * (n + 1))
                pool.tensor_tensor(sq[:, :, :, 0:4], sq[:, :, :, 0:4], sq[:, :, :, 4:8], ALU.add).then_inc(s_pool, 1)
                pool.wait_ge(s_pool, own.next())
                pool.tensor_tensor(sq[:, :, :, 0:2], sq[:, :, :, 0:2], sq[:, :, :, 2:4], ALU.add).then_inc(s_pool, 1)
                pool.wait_ge(s_pool, own.next())
                pool.tensor_tensor(feat[:, :, :, D], sq[:, :, :, 0], sq[:, :, :, 1], ALU.add).then_inc(s_ninth, 1)

            def residual(n):
                pool.wait_ge(s_first, n + 1)
                if positive(n):
                    pool.wait_ge(s_third, n)
                pool.tensor_tensor(resid[:].rearrange(flat), feat[:].rearrange(flat),
                                   parts[:, :, 0:FEAT], ALU.subtract).then_inc(s_resid, 1)

            def third_part(n):
                pool.wait_ge(s_second, n + 1)
                for a, place in ((0, 6), (1, 5)):
                    ins = pool.tensor_tensor(slots[:, a, :, place, :], resid[:, a], slots[:, a, :, 1, :],
                                             ALU.subtract)
                ins.then_inc(s_third, 1)

            def step(b, p):
                prev, cur, nxt, prep, norm = present(b)
                own.count = 0
                pool.sem_clear(s_pool)
                if norm:
                    deviation(b + 3)
                if prep:
                    variance(b + 2)
                    residual(b + 2)
                    third_part(b + 2)

            run_steps(pool, step)

            def scales(n):
                own = Own()
                pool.sem_clear(s_pool)
                var = gmv[:, :, 1]
                pool.wait_ge(s_gvar, n + 1)
                if positive(n):
                    pool.wait_ge(s_gxb, n)
                pool.tensor_tensor(gt[:], var, epsilon[:], ALU.add).then_inc(s_pool, 1)
                pool.wait_ge(s_pool, own.next())
                pool.tensor_tensor(gr1[:], gt[:], minus_half[:], ALU.pow).then_inc(s_pool, 1)
                pool.wait_ge(s_pool, own.next())
                pool.tensor_tensor(gt[:], gr1[:], gr1[:], ALU.mult).then_inc(s_pool, 1)
                pool.wait_ge(s_pool, own.next())
                pool.tensor_tensor(gt[:], gt[:], var, ALU.mult).then_inc(s_pool, 1)
                pool.wait_ge(s_pool, own.next())
                pool.tensor_tensor(gt[:], gt[:], epsilon[:], ALU.add).then_inc(s_pool, 1)
                pool.wait_ge(s_pool, own.next())
                pool.tensor_tensor(gr2[:], gt[:], minus_half[:], ALU.pow).then_inc(s_pool, 1)
                pool.wait_ge(s_pool, own.next())
                pool.tensor_tensor(gr12[:], gr1[:], gr2[:], ALU.mult).then_inc(s_gr, 1)

            def scales2(n):
                own = Own()
                pool.sem_clear(s_pool)
                pool.wait_ge(s_var2, n + 1)
                pool.tensor_tensor(rstd2[:], mv2[:, :, 1], epsilon[:], ALU.add).then_inc(s_pool, 1)
                pool.wait_ge(s_pool, own.next())
                pool.tensor_tensor(rstd2[:], rstd2[:], minus_half[:], ALU.pow).then_inc(s_rstd2, 1)

            def sum_xz(n, p):
                pool.wait_ge(s_xg[p], n * 32 + (64 - 32 * p))
                pool.wait_ge(s_zg[p], n * 32 + (64 - 32 * p))
                if positive(n - 1):
                    pool.wait_ge(s_acc0, n - 1)
                pool.tensor_tensor(xzg[p][:], xg[p][:], zg[p][:], ALU.add).then_inc(s_xzg, 1)

            def step(g, p):
                ffn, tail, head, norm = group_present(g)
                if tail:
                    scales2(g + 1)
                if norm:
                    scales(g + 3)
                    sum_xz(g + 3, 1 - p)

            run_groups(pool, step)

        @block.tensor
        def _(pe):
            pe.wait_ge(s_ident, 1)
            pe.wait_ge(s_setup, 1)
            pe.wait_ge(s_dma_w, 64)

            def mm(o, l, r, start=True, stop=True):
                return pe.matmul(o, l, r, start=start, stop=stop, skip_group_check=True)

            def misc16(m):
                return misc[m][:].bitcast(BF16)

            def xn_transposes(n, p):
                pe.wait_ge(s_xn, n + 1)
                for st in range(ST):
                    ins = pe.transpose(misc[1][:, st * P:(st + 1) * P], xn[:, st, :], ident[:])
                ins.then_inc(s_xt_ps, 1)

            def project_qk(n, p):
                pe.wait_ge(s_xt, n + 1)
                for st in range(ST):
                    ins = mm(misc[1][:, st * 256:(st + 1) * 256], xnT[p][:, st * P:(st + 1) * P],
                             wqk[:].rearrange("p a h d -> p (a h d)"))
                ins.then_inc(s_qk_ps, 1)

            def project_v(n, p):
                for st in range(ST):
                    ins = mm(misc[1][:, st * P:(st + 1) * P], xnT[p][:, st * P:(st + 1) * P], wv[:])
                ins.then_inc(s_v_ps, 1)

            def stack_transposes(n, a, k):
                m = misc16(1 if (a == 1 and k == 0) else 0)
                if a == 0:
                    pe.wait_ge(s_stack, n + 1)
                    pe.wait_ge(s_third, n + 1)
                for q in range(HP):
                    for st in range(ST):
                        h = 2 * (HP * k + q)
                        ins = pe.transpose(m[:, q * NS + st * P:q * NS + (st + 1) * P],
                                           stack[:, a, st, h:h + 2, :].rearrange("p h k -> p (h k)"), identb[:])
                ins.then_inc((s_qt_ps if a == 0 else s_kt_ps)[k], 1)

            def row_pass(n, p, h):
                if h % 8 == 0:
                    pe.wait_ge(s_qt[h // 8], n + 1)
                    pe.wait_ge(s_kt[h // 8], n + 1)
                if h == 0:
                    if positive(H * n):
                        pe.wait_ge(s_max, H * n)
                elif h >= 3:
                    pe.wait_ge(s_max, H * n + h - 2)
                q = h // 2
                for st in range(ST):
                    ins = mm(row_scores[h % 3][:, st * NS:(st + 1) * NS],
                             QT[p][:, q, st * P:(st + 1) * P], KT[p][h % 2][:, q, :])
                ins.then_inc(s_row, 1)

            def col_pass(b, p, h):
                if h % 8 == 0:
                    pe.wait_ge(s_shd[h // 8], 64 * (b + 1))
                if positive(H * b + h - 1):
                    pe.wait_ge(s_exp, H * b + h - 1)
                q = h // 2
                for tc in range(ST):
                    ins = mm(col_scores[h % 2][:, tc * NS:(tc + 1) * NS],
                             KT[p][h % 2][:, q, tc * P:(tc + 1) * P], QT[p][:, q, :])
                ins.then_inc(s_col, 1)

            def pv(b, p, g):
                pe.wait_ge(s_exp, H * b + 4 * g + 4)
                if g % 2 == 0:
                    if g == 0:
                        if positive(b):
                            pe.wait_ge(s_ot[1], b)
                    else:
                        pe.wait_ge(s_ot[0], b + 1)
                for tc in range(ST):
                    for j in range(4):
                        h = 4 * g + j
                        ins = mm(pv_bank[32 * j:32 * j + FEAT, (g % 2) * NS:(g % 2 + 1) * NS],
                                 V[p][:, tc, h, :], prob[:, h % 8, tc, :],
                                 start=(tc == 0), stop=(tc == ST - 1))
                ins.then_inc(s_pv, 1)

            def out_transposes(b, k):
                pe.wait_ge(s_ot[k], b + 1)
                for g in range(2):
                    for st in range(ST):
                        c = (g * ST + st) * P
                        ins = pe.transpose(misc[0][:, c:c + P], oT[k][:, g, st * P:(st + 1) * P], ident[:])
                ins.then_inc(s_on_ps[k], 1)

            def merge_transposes(b):
                pe.wait_ge(s_on[1], b + 1)
                for st in range(ST):
                    ins = pe.transpose(misc[0][:, st * P:(st + 1) * P],
                                       o_nat[:, st].rearrange("p h d -> p (h d)"), ident[:])
                ins.then_inc(s_oa_ps, 1)

            def project_out(b):
                pe.wait_ge(s_oa, b + 1)
                for st in range(ST):
                    ins = mm(misc[0][:, st * P:(st + 1) * P], oT_all[:, st * P:(st + 1) * P], wo[:])
                ins.then_inc(s_pr_ps, 1)

            def shift_transposes(n, k):
                pe.wait_ge(s_shift[k], n + 1)
                for st in range(ST):
                    ins = pe.transpose(misc16(1)[0:SROWS, st * P:(st + 1) * P],
                                       shift[k][:, st].rearrange("p a r q -> p (a r q)"), identb[:])
                ins.then_inc(s_sht_ps[k], 1)

            def step(b, p):
                prev, cur, nxt, prep, norm = present(b)
                for h in range(H):
                    if cur:
                        col_pass(b, p, h)
                    if h == 0 and prev:
                        pv(b - 1, 1 - p, 3)
                    if h % 4 == 1 and h > 4 and cur:
                        pv(b, p, h // 4 - 1)
                    if h == PE_AT["q1"] and nxt:
                        if prev:
                            pe.wait_ge(s_on[0], b)
                        else:
                            pe.wait_ge(s_qt[0], b + 2)
                        stack_transposes(b + 1, 0, 1)
                    if nxt:
                        row_pass(b + 1, 1 - p, h)
                    if h == PE_AT["k1"] and nxt:
                        pe.wait_ge(s_qt[1], b + 2)
                        stack_transposes(b + 1, 1, 1)
                    if h == PE_AT["out1"] and prev:
                        if nxt:
                            pe.wait_ge(s_kt[1], b + 2)
                        else:
                            pe.wait_ge(s_on[0], b)
                        out_transposes(b - 1, 1)
                    if h == PE_AT["merge"] and prev:
                        merge_transposes(b - 1)
                    if h == PE_AT["project"] and prev:
                        project_out(b - 1)
                    if h == PE_AT["q0"] and prep:
                        if prev:
                            pe.wait_ge(s_z, b)
                        elif nxt:
                            pe.wait_ge(s_kt[1], b + 2)
                        stack_transposes(b + 2, 0, 0)
                    if h == PE_AT["out0"] and cur:
                        if prep:
                            pe.wait_ge(s_qt[0], b + 3)
                        else:
                            pe.wait_ge(s_z, b)
                        out_transposes(b, 0)
                    if h == PE_AT["shift1"] and cur:
                        if prep:
                            pe.wait_ge(s_feat, 2 * (b + 3))
                        elif nxt:
                            pe.wait_ge(s_kt[0], b + 2)
                        else:
                            pe.wait_ge(s_sht[0], b + 1)
                        shift_transposes(b, 1)
                    if h == PE_AT["v"] and nxt:
                        if cur:
                            pe.wait_ge(s_sht[1], b + 1)
                        else:
                            pe.wait_ge(s_feat, 2 * (b + 3))
                        project_v(b + 1, 1 - p)
                    if h == PE_AT["x"] and norm:
                        if nxt:
                            pe.wait_ge(s_v, b + 2)
                        elif prep:
                            pe.wait_ge(s_feat, 2 * (b + 3))
                        xn_transposes(b + 3, 1 - p)
                    if h == PE_AT["shift0"] and nxt:
                        if norm:
                            pe.wait_ge(s_xt, b + 4)
                        else:
                            pe.wait_ge(s_v, b + 2)
                        shift_transposes(b + 1, 0)
                    if h == PE_AT["k0"] and prep:
                        if nxt:
                            pe.wait_ge(s_sht[0], b + 2)
                        else:
                            pe.wait_ge(s_xt, b + 4)
                        stack_transposes(b + 2, 1, 0)
                    if h == PE_AT["qk"] and norm:
                        if prep:
                            pe.wait_ge(s_kt[0], b + 3)
                        project_qk(b + 3, 1 - p)

            run_steps(pe, step)

            pe.wait_ge(s_z, NB)
            pe.wait_ge(s_ident, 2)
            pe.wait_ge(s_setup, 2)
            mm(misc[0][:, 0:E], bv_wide[:], out_wT[:]).then_inc(s_bvw, 1)

            def hn_transposes(n):
                pe.wait_ge(s_gxh, n + 1)
                if not isinstance(n, int) or n > 0:
                    pe.wait_ge(s_vexp, n)
                else:
                    pe.wait_ge(s_setup, 3)
                for t in range(TILES):
                    ins = pe.transpose(misc[0][:, t * P:(t + 1) * P], gxh[:, t, :], ident[:])
                ins.then_inc(s_hn_ps, 1)

            def causal_q(n):
                pe.wait_ge(s_hn, n + 1)
                mm(misc[0][:], in_wT[:, 0:E], hnT[:]).then_inc(s_gq_ps, 1)

            def causal_k(n):
                pe.wait_ge(s_gq, n + 1)
                mm(misc[0][:], in_wT[:, E:2 * E], hnT[:]).then_inc(s_gk_ps, 1)

            def causal_v(n):
                pe.wait_ge(s_kexp, n + 1)
                for t in range(TILES):
                    ins = mm(misc[0][:, t * P:(t + 1) * P], hnT[:, t * P:(t + 1) * P], in_wT[:, 2 * E:3 * E])
                ins.then_inc(s_gv_ps, 1)

            def causal_scores(n, t):
                if t < 2:
                    if positive(2 * (n - 1) + t + 1):
                        pe.wait_ge(s_son, 2 * (n - 1) + t + 1)
                else:
                    pe.wait_ge(s_sdiff, 4 * n + t - 1)
                m = seq_bank[t % 2]
                mm(m[:], seq_eye[:].rearrange("k n s -> k (n s)"), causal[:].rearrange("k h t -> k (h t)"),
                   stop=False)
                for q in range(QUAD):
                    c = t * P + q * SEQ
                    ins = mm(m[q * SEQ:(q + 1) * SEQ, :], gqT[:, c:c + SEQ],
                             Kexp[:, t * QUAD + q].rearrange("p h t -> p (h t)"), start=False)
                ins.then_inc(s_sc, 1)

            def causal_pv(n):
                pe.wait_ge(s_spT, 4 * (n + 1))
                pe.wait_ge(s_vexp, n + 1)
                for h in range(H):
                    c = (h % 8) * QUAD * FEAT
                    for t in range(TILES):
                        ins = mm(seq_bank[h // 8][t * SEQ:(t + 1) * SEQ, c:c + QUAD * FEAT],
                                 sprobT[:, t, h, :], Vexp[:, t, h].rearrange("p n c -> p (n c)"))
                    if h % 8 == 7:
                        ins.then_inc(s_spv, 1)

            def merged_transposes(n):
                pe.wait_ge(s_son, 2 * (n + 1))
                if positive(n):
                    pe.wait_ge(s_ld, n)
                for q in range(QUAD):
                    ins = pe.transpose(misc[1][:, q * P:(q + 1) * P], so_nat[:, q].rearrange("p h d -> p (h d)"),
                                       ident[:])
                ins.then_inc(s_a_ps, 1)

            def causal_out(n):
                pe.wait_ge(s_a, n + 1)
                for t in range(TILES):
                    ins = mm(misc[1][:, t * P:(t + 1) * P], aT[:, t].rearrange("p n s -> p (n s)"), out_wT[:])
                ins.then_inc(s_pj_ps, 1)

            def h2_transposes(n):
                pe.wait_ge(s_h2n, n + 1)
                for t in range(TILES):
                    ins = pe.transpose(misc[1][:, t * P:(t + 1) * P], h2n[:, t, :], ident[:])
                ins.then_inc(s_h2_ps, 1)

            def router_logits(n, p):
                pe.wait_ge(s_h2, n + 1)
                for t in range(TILES):
                    ins = mm(misc[1][:, t * NE:(t + 1) * NE], hn2T[p][:, t * P:(t + 1) * P], router[:])
                ins.then_inc(s_lg_ps, 1)

            def expert_up(g, p, e):
                if e == 0:
                    pe.wait_ge(s_h2, g + 1)
                for c in range(FC):
                    if positive(NE * FC * g + FC * e + c - 1):
                        pe.wait_ge(s_mid, NE * FC * g + FC * e + c - 1)
                    mm(up_bank[c][:], w1_sb[:, e, c * P:(c + 1) * P], hn2T[p][:]).then_inc(s_up, 1)

            def expert_down(g, e):
                pe.wait_ge(s_mid, NE * FC * g + FC * (e + 1))
                if positive(NE * g + e - 1):
                    pe.wait_ge(s_acc, NE * g + e - 1)
                for t in range(TILES):
                    for c in range(FC):
                        ins = mm(down_bank[e % 2][:, t * P:(t + 1) * P], hmid[e % 2][c][:, t * P:(t + 1) * P],
                                 w2_sb[:, e, c, :], start=(c == 0), stop=(c == FC - 1))
                ins.then_inc(s_dn, 1)

            def group_step(g, p):
                ffn, tail, head, norm = group_present(g)
                for e in range(NE):
                    if ffn:
                        expert_up(g, p, e)
                    if head:
                        if e == 0:
                            hn_transposes(g + 2)
                        if e == 1:
                            causal_q(g + 2)
                        if e == 2:
                            causal_k(g + 2)
                        if e == 5:
                            causal_v(g + 2)
                        if e >= 6:
                            causal_scores(g + 2, 2 * (e - 6))
                            causal_scores(g + 2, 2 * (e - 6) + 1)
                    if tail:
                        if e == 1:
                            causal_pv(g + 1)
                        if e == 2:
                            merged_transposes(g + 1)
                        if e == 3:
                            causal_out(g + 1)
                        if e == 5:
                            h2_transposes(g + 1)
                        if e == 6:
                            router_logits(g + 1, 1 - p)
                    if ffn and e > 0:
                        expert_down(g, e - 1)
                if ffn:
                    expert_down(g, NE - 1)

            run_groups(pe, group_step)

        @block.vector
        def _(dve):
            own = Own()
            for t in (*QT, *KT[0], *KT[1], stack):
                dve.memzero(t[:]).then_inc(s_dve, 1)
                dve.wait_ge(s_dve, own.next())
            for t in V:
                dve.memset(t[:], 1.0).then_inc(s_dve, 1)
                dve.wait_ge(s_dve, own.next())
            dve.memset(pv_bank[:], 0.0).then_inc(s_dve, 1)
            dve.wait_ge(s_dve, own.next())
            dve.memset(stack[:, 1, :, :, SHIFT:SHIFT + SPARTS], 1.0).then_inc(s_dve, 1)
            dve.wait_ge(s_dve, own.next())
            dve.wait_ge(s_dma_w, 64)
            dve.tensor_reduce(wqk_mean[:], wqk_raw[:].rearrange("p a h d -> p (a h) d"), AX.X, ALU.add).then_inc(s_dve, 1)
            dve.wait_ge(s_dve, own.next())
            dve.tensor_scalar(wqk_mean[:], wqk_mean[:], 1.0 / D, None, ALU.mult).then_inc(s_dve, 1)
            dve.wait_ge(s_dve, own.next())
            dve.tensor_tensor(wqk[:].rearrange("p a h d -> p (a h) d"),
                              wqk_raw[:].rearrange("p a h d -> p (a h) d"),
                              wqk_mean[:].unsqueeze(2).broadcast_to([P, 2 * H, D]),
                              ALU.subtract).then_inc(s_setup, 1)

            def x_statistics(n, p):
                dve.wait_ge(s_x[p], n * 8 + (16 - 8 * p))
                if positive(n):
                    dve.wait_ge(s_xn, n)
                for st in range(ST):
                    ins = dve.bn_stats(stats[:, st, :], x_in[p][:, st, :])
                ins.then_inc(s_dve, 1)
                dve.wait_ge(s_dve, own.next())
                for st in range(ST):
                    ins = dve.bn_aggr(mv[:, st, :], stats[:, st, :])
                ins.then_inc(s_var, 1)

            def normalise_x(n, p):
                dve.wait_ge(s_rstd, n + 1)
                if positive(n):
                    dve.wait_ge(s_xt_ps, n)
                for st in range(ST):
                    ins = dve.tensor_scalar(xn[:, st, :], x_in[p][:, st, :], mv[:, st, 0:1],
                                            rstd[:, st:st + 1], ALU.subtract, ALU.mult)
                ins.then_inc(s_xn, 1)

            def first_part(n):
                dve.wait_ge(s_ninth, n + 1)
                if positive(n):
                    dve.wait_ge(s_kt_ps[1], n)
                dve.tensor_copy(parts[:, :, 0:FEAT], feat[:].rearrange(flat)).then_inc(s_first, 1)

            def second_part(n):
                dve.wait_ge(s_resid, n + 1)
                dve.tensor_copy(parts[:, :, FEAT:2 * FEAT], resid[:].rearrange(flat)).then_inc(s_second, 1)

            def repeat_first(n):
                dve.wait_ge(s_first, n + 1)
                for a, place in ((0, 3), (1, 4)):
                    ins = dve.tensor_copy(slots[:, a, :, place:place + 3:2, :],
                                          slots[:, a, :, 0:1, :].broadcast_to([P, ST * H, 2, FEAT]))
                ins.then_inc(s_dve, 1)
                dve.wait_ge(s_dve, own.next())

            def repeat_second(n):
                dve.wait_ge(s_second, n + 1)
                for a, place in ((0, 4), (1, 3)):
                    ins = dve.tensor_copy(slots[:, a, :, place, :], slots[:, a, :, 1, :])
                ins.then_inc(s_stack, 1)

            def q_out(n, p, k):
                dve.wait_ge(s_qt_ps[k], n + 1)
                if positive(H * (n - 2) + 8 * k + 8):
                    dve.wait_ge(s_col, H * (n - 2) + 8 * k + 8)
                dve.tensor_copy(QT[p][:, HP * k:HP * (k + 1), :],
                                misc[0][:].bitcast(BF16).rearrange("p (q s) -> p q s", q=HP)).then_inc(s_qt[k], 1)

            def take_max(n, h):
                dve.wait_ge(s_row, H * n + h + 1)
                if h % 8 == 0:
                    if positive(n):
                        dve.wait_ge(s_shift[h // 8], n)
                dve.tensor_reduce(rowmax[h // 8][:, :, h % 2, h % 8 // 2],
                                  row_scores[h % 3][:].rearrange("p (s t) -> p s t", s=ST),
                                  AX.X, ALU.max).then_inc(s_max, 1)

            def negate(n, k):
                dve.wait_ge(s_max, H * n + 8 * k + 8)
                if positive(n):
                    dve.wait_ge(s_sht_ps[k], n)
                dve.tensor_scalar(shift[k][:, :, :, 0, :], rowmax[k][:], -1.0, None, ALU.mult).then_inc(s_dve, 1)
                dve.wait_ge(s_dve, own.next())
                dve.scalar_tensor_tensor(out=shift[k][:, :, :, 1, :], in0=rowmax[k][:], scalar=-1.0,
                                         in1=shift[k][:, :, :, 0, :],
                                         op0=ALU.mult, op1=ALU.subtract).then_inc(s_shift[k], 1)

            def normalise_out(b, k):
                dve.wait_ge(s_on_ps[k], b + 1)
                src = misc[0][:].rearrange("p (g s j c) -> p g s j c", g=2, s=ST, j=4)
                dve.reciprocal(rsum[k][:], src[:, :, :, :, D]).then_inc(s_dve, 1)
                dve.wait_ge(s_dve, own.next())
                if positive(b):
                    dve.wait_ge(s_oa_ps, b)
                for g in range(2):
                    ins = dve.tensor_tensor(o_nat[:, :, 8 * k + 4 * g:8 * k + 4 * g + 4, :],
                                            src[:, g, :, :, 0:D],
                                            rsum[k][:, g].unsqueeze(3).broadcast_to([P, ST, 4, D]), ALU.mult)
                ins.then_inc(s_on[k], 1)

            def take_output(b, p):
                dve.wait_ge(s_pr_ps, b + 1)
                if positive(b * 8 - 8 * p):
                    dve.wait_ge(s_zd[p], b * 8 - 8 * p)
                dve.tensor_copy(z_out[p][:].rearrange("p s e -> p (s e)"), misc[0][:, 0:NS]).then_inc(s_z, 1)

            def step(b, p):
                prev, cur, nxt, prep, norm = present(b)
                own.count = 0
                dve.sem_clear(s_dve)
                for h in range(H):
                    if h == DVE_AT["q1"] and nxt:
                        q_out(b + 1, 1 - p, 1)
                    if nxt:
                        take_max(b + 1, h)
                    if h == DVE_AT["statistics"] and norm:
                        x_statistics(b + 3, 1 - p)
                    if h == DVE_AT["normalise"] and norm:
                        normalise_x(b + 3, 1 - p)
                    if h == DVE_AT["first"] and prep:
                        first_part(b + 2)
                    if h == DVE_AT["out1"] and prev:
                        normalise_out(b - 1, 1)
                    if h == DVE_AT["second"] and prep:
                        second_part(b + 2)
                    if h == DVE_AT["shift0"] and nxt:
                        negate(b + 1, 0)
                    if h == DVE_AT["repeat1"] and prep:
                        repeat_first(b + 2)
                    if h == DVE_AT["repeat2"] and prep:
                        repeat_second(b + 2)
                    if h == DVE_AT["output"] and prev:
                        take_output(b - 1, 1 - p)
                    if h == DVE_AT["q0"] and prep:
                        q_out(b + 2, p, 0)
                    if h == DVE_AT["out0"] and cur:
                        normalise_out(b, 0)
                if nxt:
                    negate(b + 1, 1)

            run_steps(dve, step)

            own.count = 0
            dve.sem_clear(s_dve)
            dve.wait_ge(s_ident, 2)
            dve.wait_ge(s_dma_w2, 16 * 11)
            dve.tensor_copy(bv_wide[:], in_bT[:, 2:3].broadcast_to([P, P])).then_inc(s_dve, 1)
            dve.wait_ge(s_dve, own.next())
            dve.memset(Vexp[:], 0.0).then_inc(s_dve, 1)
            dve.wait_ge(s_dve, own.next())
            for q in range(QUAD):
                dve.memset(Vexp[q * SEQ:(q + 1) * SEQ, :, :, q, D:D + 1], 1.0).then_inc(s_dve, 1)
                dve.wait_ge(s_dve, own.next())
            dve.tensor_scalar(head_bias[:], head_mask[:], in_bT[:, 1:2], None, ALU.mult).then_inc(s_setup, 1)
            dve.wait_ge(s_bvw, 1)
            dve.tensor_tensor(ob_row[:], misc[0][:, 0:E], ob_raw[:], ALU.add).then_inc(s_setup, 1)

            def group_statistics(n, p):
                dve.wait_ge(s_xg[p], n * 32 + (64 - 32 * p))
                if positive(n):
                    dve.wait_ge(s_gxb, n)
                for t in range(TILES):
                    ins = dve.bn_stats(gstats[:, t, :], xg[p][:, t, :])
                ins.then_inc(s_dve, 1)
                dve.wait_ge(s_dve, own.next())
                for t in range(TILES):
                    ins = dve.bn_aggr(gmv[:, t, :], gstats[:, t, :])
                ins.then_inc(s_gvar, 1)

            def group_normalise(n, p):
                dve.wait_ge(s_gr, n + 1)
                if positive(n):
                    dve.wait_ge(s_hn_ps, n)
                for t in range(TILES):
                    ins = dve.tensor_scalar(gxh[:, t, :], xg[p][:, t, :], gmv[:, t, 0:1], gr12[:, t:t + 1],
                                            ALU.subtract, ALU.mult)
                ins.then_inc(s_gxh, 1)
                if positive(n - 1):
                    dve.wait_ge(s_xattn, n - 1)
                for t in range(TILES):
                    ins = dve.tensor_scalar(gxb[p][:, t, :], xg[p][:, t, :], gmv[:, t, 0:1], gr1[:, t:t + 1],
                                            ALU.subtract, ALU.mult)
                ins.then_inc(s_dve, 1)
                dve.wait_ge(s_dve, own.next())
                dve.tensor_tensor(gxb[p][:], gxb[p][:], ob_row[:].unsqueeze(1).broadcast_to([P, TILES, E]),
                                  ALU.add).then_inc(s_gxb, 1)

            def take_q(n):
                dve.wait_ge(s_gq_ps, n + 1)
                if positive(4 * n):
                    dve.wait_ge(s_sc, 4 * n)
                dve.tensor_scalar(gqT[:], misc[0][:], in_bT[:, 0:1], None, ALU.add).then_inc(s_gq, 1)

            def take_v(n):
                dve.wait_ge(s_gv_ps, n + 1)
                if positive(2 * n):
                    dve.wait_ge(s_spv, 2 * n)
                ps = misc[0][:].rearrange("p (t h d) -> p t h d", t=TILES, h=H)
                for q in range(QUAD):
                    rows = slice(q * SEQ, (q + 1) * SEQ)
                    ins = dve.tensor_copy(Vexp[rows, :, :, q, 0:D], ps[rows])
                ins.then_inc(s_vexp, 1)

            def score_maxima(n, t):
                ps = seq_bank[t % 2][:].rearrange("p (h t) -> p h t", h=H)
                dve.wait_ge(s_sc, 4 * n + t + 1)
                dve.tensor_reduce(smax[:, t, :], ps, AX.X, ALU.max).then_inc(s_dve, 1)
                dve.wait_ge(s_dve, own.next())
                if positive(4 * (n - 1) + t + 1):
                    dve.wait_ge(s_sprob, 4 * (n - 1) + t + 1)
                dve.tensor_tensor(sdiff[:, t], ps, smax[:, t, :].unsqueeze(2).broadcast_to([P, H, SEQ]),
                                  ALU.subtract).then_inc(s_sdiff, 1)

            def block_transposes(n):
                if positive(2 * n):
                    dve.wait_ge(s_spv, 2 * n)
                for t in range(TILES):
                    dve.wait_ge(s_sprob, 4 * n + t + 1)
                    dve.transpose(sprobT[:, t].rearrange("p h s -> p (h s)"),
                                  sprob[:, t].rearrange("p h s -> p (h s)")).then_inc(s_spT, 1)

            def causal_normalise(n):
                for k in range(2):
                    dve.wait_ge(s_spv, 2 * n + k + 1)
                    src = seq_bank[k][:, 0:8 * QUAD * FEAT].rearrange("p (h n c) -> p h n c", h=8, n=QUAD)
                    dve.reciprocal(srec[k][:], src[:, :, :, D]).then_inc(s_dve, 1)
                    dve.wait_ge(s_dve, own.next())
                    if positive(n):
                        dve.wait_ge(s_a_ps, n)
                    for q in range(QUAD):
                        ins = dve.tensor_tensor(so_nat[:, q, 8 * k:8 * k + 8, :], src[:, :, q, 0:D],
                                                srec[k][:, :, q].unsqueeze(2).broadcast_to([P, 8, D]), ALU.mult)
                    ins.then_inc(s_son, 1)

            def make_x1(n, p):
                dve.wait_ge(s_pj_ps, n + 1)
                if positive(n):
                    dve.wait_ge(s_h2n, n)
                dve.tensor_tensor(x1[:], misc[1][:].rearrange("p (t e) -> p t e", t=TILES), gxb[p][:],
                                  ALU.add).then_inc(s_xattn, 1)
                dve.wait_ge(s_xattn, n + 1)
                for t in range(TILES):
                    ins = dve.bn_stats(stats2[:, t, :], x1[:, t, :])
                ins.then_inc(s_dve, 1)
                dve.wait_ge(s_dve, own.next())
                for t in range(TILES):
                    ins = dve.bn_aggr(mv2[:, t, :], stats2[:, t, :])
                ins.then_inc(s_var2, 1)
                dve.wait_ge(s_xzg, n + 1)
                if positive(n * 32 - 32 * p):
                    dve.wait_ge(s_out[p], n * 32 - 32 * p)
                dve.tensor_tensor(acc[p][:], x1[:], xzg[p][:], ALU.add).then_inc(s_acc0, 1)

            def normalise_x1(n):
                dve.wait_ge(s_rstd2, n + 1)
                if positive(n):
                    dve.wait_ge(s_h2_ps, n)
                for t in range(TILES):
                    ins = dve.tensor_scalar(h2n[:, t, :], x1[:, t, :], mv2[:, t, 0:1], rstd2[:, t:t + 1],
                                            ALU.subtract, ALU.mult)
                ins.then_inc(s_h2n, 1)

            def choose(n):
                dve.wait_ge(s_lg_ps, n + 1)
                dve.tensor_copy(logit[:].rearrange("p t e -> p (t e)"), misc[1][:, 0:TILES * NE]).then_inc(s_dve, 1)
                dve.wait_ge(s_dve, own.next())
                for t in range(TILES):
                    ins = dve.max(top[:, t, :], logit[:, t, :])
                ins.then_inc(s_dve, 1)
                dve.wait_ge(s_dve, own.next())
                if positive(n):
                    dve.wait_ge(s_le, n)
                dve.tensor_tensor(ldiff[:], logit[:], top[:, :, 0:1].broadcast_to([P, TILES, NE]),
                                  ALU.subtract).then_inc(s_ld, 1)
                for t in range(TILES):
                    ins = dve.max_index(topi[:, t, :], top[:, t, :], logit[:, t, :])
                ins.then_inc(s_dve, 1)
                dve.wait_ge(s_dve, own.next())
                dve.tensor_copy(topf[:], topi[:, :, 0:2]).then_inc(s_dve, 1)
                dve.wait_ge(s_dve, own.next())
                for k in range(2):
                    ins = dve.tensor_tensor(pick[:, k], index8[:], topf[:, :, k:k + 1].broadcast_to([P, TILES, NE]),
                                            ALU.is_equal)
                ins.then_inc(s_dve, 1)
                dve.wait_ge(s_dve, own.next())
                dve.tensor_tensor(pick[:, 0], pick[:, 0], pick[:, 1], ALU.add).then_inc(s_dve, 1)
                dve.wait_ge(s_dve, own.next())

            def make_gates(n, p):
                dve.wait_ge(s_le, n + 1)
                dve.tensor_reduce(lsum[:], lexp[:], AX.X, ALU.add).then_inc(s_dve, 1)
                dve.wait_ge(s_dve, own.next())
                dve.reciprocal(lsum[:], lsum[:]).then_inc(s_dve, 1)
                dve.wait_ge(s_dve, own.next())
                dve.tensor_tensor(gate[p][:], lexp[:], pick[:, 0], ALU.mult).then_inc(s_dve, 1)
                dve.wait_ge(s_dve, own.next())
                dve.tensor_tensor(gate[p][:], gate[p][:], lsum[:].unsqueeze(2).broadcast_to([P, TILES, NE]),
                                  ALU.mult).then_inc(s_gate, 1)

            def add_expert(g, p, e):
                if e == 0:
                    dve.wait_ge(s_gate, g + 1)
                    dve.wait_ge(s_acc0, g + 1)
                dve.wait_ge(s_dn, NE * g + e + 1)
                if positive(NE * g + e):
                    dve.wait_ge(s_acc, NE * g + e)
                for t in range(TILES):
                    ins = dve.scalar_tensor_tensor(out=acc[p][:, t, :], in0=down_bank[e % 2][:, t * P:(t + 1) * P],
                                                   scalar=gate[p][:, t, e:e + 1], in1=acc[p][:, t, :],
                                                   op0=ALU.mult, op1=ALU.add)
                ins.then_inc(s_acc, 1)

            def group_step(g, p):
                ffn, tail, head, norm = group_present(g)
                own.count = 0
                dve.sem_clear(s_dve)
                for e in range(NE):
                    if e == 0 and tail:
                        block_transposes(g + 1)
                    if head:
                        if e == 1:
                            take_q(g + 2)
                        if e == 5:
                            take_v(g + 2)
                        if e >= 6:
                            score_maxima(g + 2, 2 * (e - 6))
                            score_maxima(g + 2, 2 * (e - 6) + 1)
                    if tail:
                        if e == 1:
                            causal_normalise(g + 1)
                        if e == 3:
                            make_x1(g + 1, 1 - p)
                        if e == 4:
                            normalise_x1(g + 1)
                        if e == 6:
                            choose(g + 1)
                    if ffn and e > 0:
                        add_expert(g, p, e - 1)
                    if e == 4 and norm:
                        group_statistics(g + 3, 1 - p)
                    if e == 7 and norm:
                        group_normalise(g + 3, 1 - p)
                if tail:
                    make_gates(g + 1, 1 - p)
                if ffn:
                    add_expert(g, p, NE - 1)

            run_groups(dve, group_step)

        @block.scalar
        def _(act):
            def copy_out(b, k):
                act.wait_ge(s_pv, 4 * b + 2 * k + 2)
                if positive(b):
                    act.wait_ge(s_on_ps[k], b)
                act.copy(oT[k][:].rearrange("p g s -> p (g s)"), pv_bank[:]).then_inc(s_ot[k], 1)

            def x_out(n, p):
                act.wait_ge(s_xt_ps, n + 1)
                if positive(n - 1):
                    act.wait_ge(s_v_ps, n - 1)
                act.copy(xnT[p][:], misc[1][:, 0:NS]).then_inc(s_xt, 1)

            def features(n):
                act.wait_ge(s_qk_ps, n + 1)
                if positive(n):
                    act.wait_ge(s_resid, n)
                ps = misc[1][:].rearrange("p (s a h d) -> p a s h d", s=ST, a=2, h=H)
                for a in range(2):
                    ins = act.copy(feat[:, a, :, 0:D].rearrange("p (s h) d -> p s h d", s=ST), ps[:, a])
                ins.then_inc(s_feat, 1)
                for a in range(2):
                    ins = act.activation(sq[:, a].rearrange("p (s h) d -> p s h d", s=ST), ps[:, a], ACT.Square,
                                         scale=(D - 1) ** -0.5)
                ins.then_inc(s_feat, 1)

            def merged_out(b):
                act.wait_ge(s_oa_ps, b + 1)
                if positive(b):
                    act.wait_ge(s_pr_ps, b)
                act.copy(oT_all[:], misc[0][:, 0:NS]).then_inc(s_oa, 1)

            def v_out(n, p):
                act.wait_ge(s_v_ps, n + 1)
                if positive(4 * (n - 1)):
                    act.wait_ge(s_pv, 4 * (n - 1))
                act.copy(V[p][:, :, :, 0:D],
                         misc[1][:, 0:NS].rearrange("p (s h d) -> p s h d", s=ST, h=H)).then_inc(s_v, 1)

            def k_out(n, p, k, a):
                if a == 0:
                    act.wait_ge(s_kt_ps[k], n + 1)
                    if positive(H * (n - 2) + 8 * k + 8):
                        act.wait_ge(s_col, H * (n - 2) + 8 * k + 8)
                ps = misc[1 - k][:].bitcast(BF16).rearrange("p (q s) -> p q s", q=HP)
                half = slice(HP * k, HP * (k + 1))
                rows = slice(a * STACK, (a + 1) * STACK)
                ins = act.copy(KT[p][a][rows, half, :], ps[rows])
                if a == 1:
                    ins.then_inc(s_kt[k], 1)

            def probabilities(b, h):
                act.wait_ge(s_col, H * b + h + 1)
                if h % 4 == 0:
                    if positive(4 * b + h // 4 - 1):
                        act.wait_ge(s_pv, 4 * b + h // 4 - 1)
                act.activation(prob[:, h % 8].rearrange("p t s -> p (t s)"), col_scores[h % 2][:], ACT.Exp,
                               scale=1.0 / D).then_inc(s_exp, 1)

            def shift_out(n, k):
                act.wait_ge(s_sht_ps[k], n + 1)
                if positive(64 * n):
                    act.wait_ge(s_shd[k], 64 * n)
                act.copy(shiftT[k][:], misc[1][:].bitcast(BF16)[0:SROWS, 0:NS]).then_inc(s_sht[k], 1)

            def step(b, p):
                prev, cur, nxt, prep, norm = present(b)
                for h in range(H):
                    if cur:
                        probabilities(b, h)
                    if h == ACT_AT["copy_out1"] and prev:
                        copy_out(b - 1, 1)
                    if h == ACT_AT["features"] and prep:
                        features(b + 2)
                    if h == ACT_AT["shift1"] and cur:
                        shift_out(b, 1)
                    if nxt:
                        for a in range(2):
                            if h == ACT_AT["k1"] + a:
                                k_out(b + 1, 1 - p, 1, a)
                    if h == ACT_AT["v"] and nxt:
                        v_out(b + 1, 1 - p)
                    if h == ACT_AT["x"] and norm:
                        x_out(b + 3, 1 - p)
                    if h == ACT_AT["merged"] and prev:
                        merged_out(b - 1)
                    if h == ACT_AT["shift0"] and nxt:
                        shift_out(b + 1, 0)
                    if h == ACT_AT["copy_out0"] and cur:
                        copy_out(b, 0)
                    if prep:
                        for a in range(2):
                            if h == ACT_AT["k0"] + a:
                                k_out(b + 2, p, 0, a)

            run_steps(act, step)

            act.wait_ge(s_setup, 2)

            def hn_out(n):
                act.wait_ge(s_hn_ps, n + 1)
                if positive(n):
                    act.wait_ge(s_gv_ps, n)
                act.activation(hnT[:], misc[0][:], ACT.Identity, bias=ln1b[:, 0:1],
                               scale=ln1w[:, 0:1]).then_inc(s_hn, 1)

            def expand_k(n, lo, hi):
                if lo == 0:
                    act.wait_ge(s_gk_ps, n + 1)
                    if positive(4 * n):
                        act.wait_ge(s_sc, 4 * n)
                for h in range(lo, hi):
                    ins = act.activation(Kexp[:, :, h, :], misc[0][:].rearrange("p (n t) -> p n t", n=GPOS),
                                         ACT.Identity, bias=head_bias[:, h:h + 1], scale=head_mask[:, h:h + 1])
                if hi == H:
                    ins.then_inc(s_kexp, 1)

            def causal_exp(n, t):
                act.wait_ge(s_sdiff, 4 * n + t + 1)
                if positive(4 * (n - 1) + t + 1):
                    act.wait_ge(s_spT, 4 * (n - 1) + t + 1)
                act.activation(sprob[:, t], sdiff[:, t], ACT.Exp, scale=float(D) ** -0.5).then_inc(s_sprob, 1)

            def merged_rows(n):
                act.wait_ge(s_a_ps, n + 1)
                if positive(n):
                    act.wait_ge(s_pj_ps, n)
                act.copy(aT[:], misc[1][:].rearrange("p (n t s) -> p t n s", n=QUAD, t=TILES)).then_inc(s_a, 1)

            def h2_out(n, p):
                act.wait_ge(s_h2_ps, n + 1)
                if positive(NE * FC * (n - 1)):
                    act.wait_ge(s_up, NE * FC * (n - 1))
                act.activation(hn2T[p][:], misc[1][:], ACT.Identity, bias=ln2b[:, 0:1],
                               scale=ln2w[:, 0:1]).then_inc(s_h2, 1)

            def router_exp(n):
                act.wait_ge(s_ld, n + 1)
                if positive(n):
                    act.wait_ge(s_gate, n)
                act.activation(lexp[:], ldiff[:], ACT.Exp).then_inc(s_le, 1)

            def hidden(g, e):
                for c in range(FC):
                    act.wait_ge(s_up, NE * FC * g + FC * e + c + 1)
                    if c == 0:
                        if positive(NE * g + e - 1):
                            act.wait_ge(s_dn, NE * g + e - 1)
                    act.activation(hmid[e % 2][c][:], up_bank[c][:], ACT.Gelu).then_inc(s_mid, 1)

            def group_step(g, p):
                ffn, tail, head, norm = group_present(g)
                for e in range(NE):
                    if ffn:
                        hidden(g, e)
                    if head:
                        if e == 0:
                            hn_out(g + 2)
                        if 2 <= e < 5:
                            expand_k(g + 2, (0, 6, 12)[e - 2], (6, 12, H)[e - 2])
                    if tail:
                        if e == 2:
                            merged_rows(g + 1)
                        if e == 5:
                            h2_out(g + 1, 1 - p)
                if tail:
                    router_exp(g + 1)
                if head:
                    for t in range(TILES):
                        causal_exp(g + 2, t)

            run_groups(act, group_step)

        @block.sync
        def _(sp):
            def load_x(b, p):
                if positive(b - 1):
                    sp.wait_ge(s_xn, b - 1)
                sp.dma_start(x_in[p][:], x[b].rearrange("(s p) e -> p s e", p=P)).then_inc(s_x[p], 16)

            def place_shift(n, p, k):
                sp.wait_ge(s_sht[k], n + 1)
                for a in range(2):
                    for r in range(SPARTS):
                        row, src = STACK * a + SHIFT + r, (a * SPARTS + r) * HP
                        sp.dma_start(QT[p][row:row + 1, HP * k:HP * (k + 1), :],
                                     shiftT[k][src:src + HP, :]).then_inc(s_shd[k], 16)

            def store_z(b, p):
                sp.wait_ge(s_z, b + 1)
                sp.dma_start(z_dram[b].rearrange("(s p) e -> p s e", p=P), z_out[p][:]).then_inc(s_zd[p], 16)

            def step(b, p):
                prev, cur, nxt, prep, norm = present(b)
                if cur:
                    place_shift(b, p, 1)
                if prev:
                    store_z(b - 1, 1 - p)
                if nxt:
                    place_shift(b + 1, 1 - p, 0)
                if norm and not (isinstance(b, int) and b + 4 >= NB):
                    load_x(b + 4, p)

            load_x(0, 0)
            run_steps(sp, step)
            for p in range(2):
                sp.wait_ge(s_zd[p], 16 * NB // 2)

            def rows(a, n, q):
                return a.rearrange("b (g t q) e -> g q b t e", t=TILES, q=QUAD)[n, q]

            def load_group(n, p):
                if positive(n - 1):
                    sp.wait_ge(s_gxb, n - 1)
                if positive(n - 1):
                    sp.wait_ge(s_xzg, n - 1)
                for q in range(QUAD):
                    sp.dma_start(xg[p][q * SEQ:(q + 1) * SEQ], rows(x, n, q)).then_inc(s_xg[p], 16)
                for q in range(QUAD):
                    sp.dma_start(zg[p][q * SEQ:(q + 1) * SEQ], rows(z_dram, n, q)).then_inc(s_zg[p], 16)

            def group_step(g, p):
                ffn, tail, head, norm = group_present(g)
                if norm:
                    load_group(g + 3, 1 - p)
                if ffn:
                    sp.wait_ge(s_acc, NE * (g + 1))
                    for q in range(QUAD):
                        sp.dma_start(rows(out, g, q), acc[p][q * SEQ:(q + 1) * SEQ]).then_inc(s_out[p], 16)

            run_groups(sp, group_step)
            for p in range(2):
                sp.wait_ge(s_out[p], 64 * GROUPS // 2)


_INS = ['L0_attn_x', 'L0_attn_Wq', 'L0_attn_Wk', 'L0_attn_Wv', 'L0_attn_Wo', 'L0_ffn_ln1_w', 'L0_ffn_ln1_b',
        'L0_ffn_in_proj_w', 'L0_ffn_in_proj_b', 'L0_ffn_out_proj_w', 'L0_ffn_out_proj_b', 'L0_ffn_ln2_w',
        'L0_ffn_ln2_b', 'L0_ffn_router_w', 'L0_ffn_w1', 'L0_ffn_w2']
_TRANSPOSED = ('L0_ffn_in_proj_w', 'L0_ffn_out_proj_w', 'L0_ffn_router_w')


def kernel(**inputs):
    import numpy as _np
    import concourse.bacc as _bacc
    from concourse import mybir as _mybir
    from concourse.bass_utils import run_bass_kernel_spmd as _run

    nc = _bacc.Bacc("TRN2", target_bir_lowering=False, num_devices=1)
    arrays, args = {}, []
    for name in _INS:
        a = _np.asarray(inputs[name])
        a = _np.ascontiguousarray(a.T if name in _TRANSPOSED else a)
        arrays[f"in_{name}"] = a
        args.append(nc.dram_tensor(f"in_{name}", a.shape, _mybir.dt.from_np(a.dtype), kind="ExternalInput").ap())
    out = nc.dram_tensor("out_0", (NB, NS, E), F32, kind="ExternalOutput").ap()
    attention_and_experts_kernel(nc, *args, out)
    r = _run(nc, [arrays], core_ids=[0])
    return r.results[0]["out_0"]
```

```python
from contextlib import ExitStack

import concourse.bass as bass
from concourse import mybir

F32 = mybir.dt.float32
BF16 = mybir.dt.bfloat16
F16 = mybir.dt.float16
U32 = mybir.dt.uint32
ALU = mybir.AluOpType
ACT = mybir.ActivationFunctionType
AX = mybir.AxisListType

P = 128
NB, NS, E = 32, 256, 128
H = 16
D = E // H
EPS = 1e-5
ST = NS // P

FEAT = D + 1
STACK = 64
SHIFT = 2 * FEAT
SPARTS = 2
PAIRS = H // 2
HP = PAIRS // 2
SROWS = 2 * SPARTS * HP

PE_AT = dict(q1=1, k1=3, out1=6, merge=9, project=10, q0=12, out0=15, shift1=1, v=3, x=9, shift0=10,
             k0=12, qk=15)
DVE_AT = dict(q1=1, statistics=0, first=6, repeat1=9, out1=6, second=8, shift0=7, repeat2=8, q0=10,
              out0=15)
ACT_AT = dict(copy_out1=1, features=0, shift1=1, k1=3, v=5, x=9, merged=8, shift0=10, output=10,
              copy_out0=10, k0=12)

PE_G = dict(hn=0, q=2, k=4, v=12, pv=4, scores0=14, scores1=14, scores2=15, scores3=15, merge=6, out=9,
            h2=12, router=14)
DVE_G = dict(spT=2, q=1, seq_out=3, x1=8, h2=8, v=11, split=12, max0=14, max1=14, max2=14, max3=14,
             choose=14, statistics=7, normalise=14)
ACT_G = dict(hn=0, k0=3, k1=4, k2=5, k3=5, k4=7, k5=7, k6=9, k7=10, merged=7, h2=12)

PE_FIRST = dict(hn=0, q=3, k=5, v=15, scores0=16, scores1=17, scores2=18, scores3=19)
DVE_FIRST = dict(statistics0=-6, normalise0=-1, q=4, statistics1=8, normalise1=14, v=16,
                 max0=17, max1=18, max2=19, max3=20)
ACT_FIRST = dict(hn=1, k0=6, exp0=18, exp1=19, exp2=20, exp3=21)

TILES = 4
QUAD = 4
SEQ = 32
GPOS = TILES * QUAD
GROUPS = NS // GPOS
TOK = TILES * P
NE, FF = 8, 256
FC = FF // P
MASKED = -1.0e30
HN2_TOP, W1_TOP = 2.0 ** 8, 2.0 ** 14


def positive(count):
    return not isinstance(count, int) or count > 0


def present(b):
    if not isinstance(b, int):
        return (True,) * 5
    return tuple(0 <= b + d < NB for d in range(-1, 4))


def run_steps(eng, step, before={}):
    for b in range(-3, 3):
        if b in before:
            before[b]()
        step(b, b % 2)
    with eng.Fori(0, NB // 2 - 4) as i:
        step(2 * i + 3, 1)
        step(2 * i + 4, 0)
    for b in range(NB - 5, NB + 1):
        if b in before:
            before[b]()
        step(b, b % 2)


def first_slot(b, h):
    return (b - (NB - 1)) * H + h if isinstance(b, int) else None


def group_present(g):
    if not isinstance(g, int):
        return (True,) * 4
    return tuple(0 <= g + d < GROUPS for d in range(4))


def run_groups(eng, step):
    for g in range(-1, 1):
        step(g, g % 2)
    with eng.Fori(0, GROUPS // 2 - 2) as i:
        step(2 * i + 1, 1)
        step(2 * i + 2, 0)
    for g in range(GROUPS - 3, GROUPS):
        step(g, g % 2)


class Own:

    def __init__(self):
        self.count = 0

    def next(self):
        self.count += 1
        return self.count


def attention_and_experts_kernel(nc, x, Wq, Wk, Wv, Wo, ln1_w, ln1_b, in_w_t, in_b, out_w_t, out_b,
                                 ln2_w, ln2_b, router_t, w1, w2, out):
    ctx = ExitStack()
    with ctx:
        def sb(name, shape, dt=F32):
            return ctx.enter_context(nc.sbuf_tensor(name, shape, dt))

        def sem(name):
            return ctx.enter_context(nc.semaphore(name))

        z_dram = nc.dram_tensor("z_scratch", (NB, NS, E), F32).ap()

        bank = [ctx.enter_context(nc.psum_tensor(f"bank{i}", [P, 512], F32)) for i in range(8)]
        row_scores = bank[0:3]
        col_scores = bank[3:5]
        pv_bank = bank[5]
        misc = bank[6:8]
        up_bank, down_bank, seq_bank = bank[0:2], bank[2:4], bank[4:6]

        def head_bank(n):
            return bank[0] if isinstance(n, int) and n == 0 else misc[0]

        def score_bank(n, t):
            return bank[1 + t % 2] if isinstance(n, int) and n == 0 else seq_bank[t % 2]

        ident = sb("ident", [P, P])
        identb = sb("identb", [P, P], BF16)
        wqk = sb("wqk", [P, 2, H, D])
        wqk_raw = sb("wqk_raw", [P, 2, H, D])
        wqk_mean = sb("wqk_mean", [P, 2 * H])
        wv = sb("wv", [P, E])
        wo = sb("wo", [P, E])

        x_in = [sb(f"x_in{p}", [P, ST, E]) for p in range(2)]
        stats = sb("stats", [P, ST, 6])
        mv = sb("mv", [P, ST, 2])
        rstd = sb("rstd", [P, ST])
        minus_half = sb("minus_half", [P, TILES])
        epsilon = sb("epsilon", [P, TILES])
        xn = sb("xn", [P, ST, E])
        xnT = [sb(f"xnT{p}", [P, NS]) for p in range(2)]
        feat = sb("feat", [P, 2, ST * H, FEAT])
        resid = sb("resid", [P, 2, ST * H, FEAT])
        sq = sb("sq", [P, 2, ST * H, D])
        stack = sb("stack", [P, 2, ST, H, STACK], BF16)
        flat = "p a g k -> p (a g) k"
        parts = stack[:].rearrange("p a s h k -> p (a s h) k")
        slots = stack[:, :, :, :, 0:7 * FEAT].rearrange("p a s h (m k) -> p a (s h) m k", k=FEAT)
        QT = [sb(f"QT{p}", [P, PAIRS, NS], BF16) for p in range(2)]
        KT = [[sb(f"KT{p}_{a}", [P, PAIRS, NS], BF16) for a in range(2)] for p in range(2)]
        V = [sb(f"V{p}", [P, ST, H, FEAT]) for p in range(2)]
        rowmax = [sb(f"rowmax{k}", [P, ST, 2, HP]) for k in range(2)]
        shift = [sb(f"shift{k}", [P, ST, 2, SPARTS, HP], BF16) for k in range(2)]
        shiftT = [sb(f"shiftT{k}", [SROWS, NS], BF16) for k in range(2)]
        prob = sb("prob", [P, 8, ST, NS])
        oT = [sb(f"oT{k}", [P, 2, NS]) for k in range(2)]
        rsum = [sb(f"rsum{k}", [P, 2, ST, 4]) for k in range(2)]
        o_nat = sb("o_nat", [P, ST, H, D])
        oT_all = sb("oT_all", [P, NS])
        z_out = [sb(f"z_out{p}", [P, ST, E]) for p in range(2)]

        in_wT = sb("in_wT", [P, 3 * E])
        in_bT = sb("in_bT", [P, 3])
        out_wT = sb("out_wT", [P, E])
        ob_raw = sb("ob_raw", [P, E])
        ob_row = sb("ob_row", [P, E])
        bv_wide = sb("bv_wide", [P, P])
        ones = sb("ones", [P, P])
        ln1w, ln1b, ln2w, ln2b = (sb(n, [P, 1]) for n in ("ln1w", "ln1b", "ln2w", "ln2b"))
        router = sb("router", [P, NE])
        w1_sb = sb("w1_sb", [P, NE, FF])
        w2_sb = sb("w2_sb", [P, NE, FC, E])
        head_mask = sb("head_mask", [P, H])
        head_bias = sb("head_bias", [P, H])
        seq_eye = sb("seq_eye", [SEQ, QUAD, SEQ], BF16)
        causal = sb("causal", [SEQ, H, SEQ], BF16)
        index8 = sb("index8", [P, TILES, NE])
        xg = [sb(f"xg{p}", [P, TILES, E]) for p in range(2)]
        zg = [sb(f"zg{p}", [P, TILES, E]) for p in range(2)]
        xzg = [sb(f"xzg{p}", [P, TILES, E]) for p in range(2)]
        gstats = sb("gstats", [P, TILES, 6])
        gmv = sb("gmv", [P, TILES, 2])
        gr1 = sb("gr1", [P, TILES])
        gr2 = sb("gr2", [P, TILES])
        gr12 = sb("gr12", [P, TILES])
        gt = sb("gt", [P, TILES])
        gxh = sb("gxh", [P, TILES, E])
        gxb = [sb(f"gxb{p}", [P, TILES, E]) for p in range(2)]
        hnT = sb("hnT", [P, TOK])
        gqT = sb("gqT", [P, TOK])
        Kexp = sb("Kexp", [P, GPOS, H, SEQ])
        Vexp = sb("Vexp", [P, TILES, H, QUAD, FEAT])
        smax = sb("smax", [P, TILES, H])
        sdiff = prob[:, 0:4].rearrange("p t s (h k) -> p t (s h) k", k=SEQ)
        sprob = prob[:, 4:8].rearrange("p t s (h k) -> p t (s h) k", k=SEQ)
        sprobT = sb("sprobT", [P, TILES, H, SEQ])
        srec = [sb(f"srec{k}", [P, H // 2, QUAD]) for k in range(2)]
        so_nat = sb("so_nat", [P, QUAD, H, D])
        aT = sb("aT", [P, TILES, QUAD, SEQ])
        x1 = sb("x1", [P, TILES, E])
        stats2 = sb("stats2", [P, TILES, 6])
        mv2 = sb("mv2", [P, TILES, 2])
        rstd2 = sb("rstd2", [P, TILES])
        h2n = sb("h2n", [P, TILES, E])
        hn2T = sb("hn2T", [P, TOK])
        hn2_hi = [sb(f"hn2_hi{p}", [P, TOK], F16) for p in range(2)]
        hn2_lo = [sb(f"hn2_lo{p}", [P, TOK], F16) for p in range(2)]
        w1_hi = sb("w1_hi", [P, NE, FF], F16)
        w1_lo = sb("w1_lo", [P, NE, FF], F16)
        bound = sb("bound", [P, 1])
        hn2_scale = sb("hn2_scale", [P, 1])
        w1_max = sb("w1_max", [P, 1])
        w1_sum = sb("w1_sum", [P, 1])
        w1_scale = sb("w1_scale", [P, 1])
        up_scale = sb("up_scale", [P, 1])
        logit = sb("logit", [P, TILES, NE])
        top = sb("top", [P, TILES, 8])
        topi = sb("topi", [P, TILES, 8], U32)
        topf = sb("topf", [P, TILES, 2])
        pick = sb("pick", [P, 2, TILES, NE])
        ldiff = sb("ldiff", [P, TILES, NE])
        lexp = sb("lexp", [P, TILES, NE])
        lsum = sb("lsum", [P, TILES])
        gate = [sb(f"gate{p}", [P, TILES, NE]) for p in range(2)]
        hmid = [[sb(f"hmid{k}_{c}", [P, TOK]) for c in range(FC)] for k in range(2)]
        acc = [sb(f"acc{p}", [P, TILES, E]) for p in range(2)]

        s_dma_w = sem("s_dma_w")
        s_dma_w2 = sem("s_dma_w2")
        s_ident = sem("s_ident")
        s_pool = sem("s_pool")
        s_setup = sem("s_setup")
        s_vones = sem("s_vones")
        s_zeroed = sem("s_zeroed")
        s_bvw = sem("s_bvw")
        s_dve = sem("s_dve")
        s_x = [sem(f"s_x{p}") for p in range(2)]
        s_var = sem("s_var")
        s_xn = sem("s_xn")
        s_xt_ps = sem("s_xt_ps")
        s_xt = sem("s_xt")
        s_qk_ps = sem("s_qk_ps")
        s_feat = sem("s_feat")
        s_v_ps = sem("s_v_ps")
        s_v = sem("s_v")
        s_ninth = sem("s_ninth")
        s_first = sem("s_first")
        s_resid = sem("s_resid")
        s_second = sem("s_second")
        s_third = sem("s_third")
        s_stack = sem("s_stack")
        s_qt_ps, s_qt, s_kt_ps, s_kt = ([sem(f"{n}{k}") for k in range(2)] for n in
                                        ("s_qt_ps", "s_qt", "s_kt_ps", "s_kt"))
        s_shift = [sem(f"s_shift{k}") for k in range(2)]
        s_sht_ps = [sem(f"s_sht_ps{k}") for k in range(2)]
        s_sht = [sem(f"s_sht{k}") for k in range(2)]
        s_shd = [sem(f"s_shd{k}") for k in range(2)]
        s_ot = [sem(f"s_ot{k}") for k in range(2)]
        s_on_ps = [sem(f"s_on_ps{k}") for k in range(2)]
        s_on = [sem(f"s_on{k}") for k in range(2)]
        s_row = sem("s_row")
        s_max = sem("s_max")
        s_col = sem("s_col")
        s_exp = sem("s_exp")
        s_pv = sem("s_pv")
        s_oa_ps = sem("s_oa_ps")
        s_oa = sem("s_oa")
        s_pr_ps = sem("s_pr_ps")
        s_z = sem("s_z")
        s_zd = [sem(f"s_zd{p}") for p in range(2)]

        s_xg = [sem(f"s_xg{p}") for p in range(2)]
        s_zg = [sem(f"s_zg{p}") for p in range(2)]
        s_xzg = sem("s_xzg")
        s_gvar = sem("s_gvar")
        s_gr = sem("s_gr")
        s_gxh = sem("s_gxh")
        s_gxb = sem("s_gxb")
        s_hn_ps = sem("s_hn_ps")
        s_hn = sem("s_hn")
        s_gq_ps = sem("s_gq_ps")
        s_gq = sem("s_gq")
        s_gk_ps = sem("s_gk_ps")
        s_kexp = sem("s_kexp")
        s_gv_ps = sem("s_gv_ps")
        s_vexp = sem("s_vexp")
        s_sc = sem("s_sc")
        s_sdiff = sem("s_sdiff")
        s_sprob = sem("s_sprob")
        s_spT = sem("s_spT")
        s_spv = sem("s_spv")
        s_son = sem("s_son")
        s_a_ps = sem("s_a_ps")
        s_a = sem("s_a")
        s_pj_ps = sem("s_pj_ps")
        s_xattn = sem("s_xattn")
        s_var2 = sem("s_var2")
        s_rstd2 = sem("s_rstd2")
        s_h2n = sem("s_h2n")
        s_h2_ps = sem("s_h2_ps")
        s_h2 = sem("s_h2")
        s_lg_ps = sem("s_lg_ps")
        s_ld = sem("s_ld")
        s_le = sem("s_le")
        s_gate = sem("s_gate")
        s_split = sem("s_split")
        s_up = sem("s_up")
        s_mid = sem("s_mid")
        s_dn = sem("s_dn")
        s_acc = sem("s_acc")
        s_acc0 = sem("s_acc0")
        s_out = [sem(f"s_out{p}") for p in range(2)]

        block = ctx.enter_context(nc.Block())

        @block.gpsimd
        def _(pool):
            own = Own()
            pool.memset(minus_half[:], -0.5).then_inc(s_pool, 1)
            pool.wait_ge(s_pool, own.next())
            pool.memset(epsilon[:], EPS).then_inc(s_pool, 1)
            pool.wait_ge(s_pool, own.next())
            pool.memset(ident[:], 0.0).then_inc(s_pool, 1)
            pool.wait_ge(s_pool, own.next())
            pool.affine_select(out=ident[:], in_=ident[:], compare_op=ALU.not_equal, fill=1.0,
                               base=0, pattern=[[-1, P]], channel_multiplier=1).then_inc(s_pool, 1)
            pool.wait_ge(s_pool, own.next())
            pool.tensor_copy(identb[:], ident[:]).then_inc(s_ident, 1)
            def normalise_x(n, p):
                pool.wait_ge(s_var, n + 1)
                if positive(n):
                    pool.wait_ge(s_xt_ps, n)
                pool.tensor_tensor(rstd[:], mv[:, :, 1], epsilon[:, 0:ST], ALU.add).then_inc(s_pool, 1)
                pool.wait_ge(s_pool, own.next())
                pool.tensor_tensor(rstd[:], rstd[:], minus_half[:, 0:ST], ALU.pow).then_inc(s_pool, 1)
                pool.wait_ge(s_pool, own.next())
                for st in range(ST):
                    ins = pool.tensor_scalar(xn[:, st, :], x_in[p][:, st, :], mv[:, st, 0:1],
                                             rstd[:, st:st + 1], ALU.subtract, ALU.mult)
                ins.then_inc(s_xn, 1)

            def variance(n):
                pool.wait_ge(s_feat, 2 * (n + 1))
                pool.tensor_tensor(sq[:, :, :, 0:4], sq[:, :, :, 0:4], sq[:, :, :, 4:8],
                                   ALU.add).then_inc(s_pool, 1)
                pool.wait_ge(s_pool, own.next())
                pool.tensor_tensor(sq[:, :, :, 0:2], sq[:, :, :, 0:2], sq[:, :, :, 2:4],
                                   ALU.add).then_inc(s_pool, 1)
                pool.wait_ge(s_pool, own.next())
                pool.tensor_tensor(feat[:, :, :, D], sq[:, :, :, 0], sq[:, :, :, 1], ALU.add).then_inc(s_ninth, 1)

            def residual(n):
                pool.wait_ge(s_first, n + 1)
                if positive(n):
                    pool.wait_ge(s_third, n)
                pool.tensor_tensor(resid[:].rearrange(flat), feat[:].rearrange(flat),
                                   parts[:, :, 0:FEAT], ALU.subtract).then_inc(s_resid, 1)

            def third_part(n):
                pool.wait_ge(s_second, n + 1)
                for a, place in ((0, 6), (1, 5)):
                    ins = pool.tensor_tensor(slots[:, a, :, place, :], resid[:, a], slots[:, a, :, 1, :],
                                             ALU.subtract)
                ins.then_inc(s_third, 1)

            def scales(n):
                var = gmv[:, :, 1]
                pool.wait_ge(s_gvar, n + 1)
                if positive(n):
                    pool.wait_ge(s_gxb, n)
                pool.tensor_tensor(gt[:], var, epsilon[:], ALU.add).then_inc(s_pool, 1)
                pool.wait_ge(s_pool, own.next())
                pool.tensor_tensor(gr1[:], gt[:], minus_half[:], ALU.pow).then_inc(s_pool, 1)
                pool.wait_ge(s_pool, own.next())
                pool.tensor_tensor(gt[:], gr1[:], gr1[:], ALU.mult).then_inc(s_pool, 1)
                pool.wait_ge(s_pool, own.next())
                pool.tensor_tensor(gt[:], gt[:], var, ALU.mult).then_inc(s_pool, 1)
                pool.wait_ge(s_pool, own.next())
                pool.tensor_tensor(gt[:], gt[:], epsilon[:], ALU.add).then_inc(s_pool, 1)
                pool.wait_ge(s_pool, own.next())
                pool.tensor_tensor(gr2[:], gt[:], minus_half[:], ALU.pow).then_inc(s_pool, 1)
                pool.wait_ge(s_pool, own.next())
                pool.tensor_tensor(gr12[:], gr1[:], gr2[:], ALU.mult).then_inc(s_gr, 1)

            def scales2(n):
                pool.wait_ge(s_var2, n + 1)
                pool.tensor_tensor(rstd2[:], mv2[:, :, 1], epsilon[:], ALU.add).then_inc(s_pool, 1)
                pool.wait_ge(s_pool, own.next())
                pool.tensor_tensor(rstd2[:], rstd2[:], minus_half[:], ALU.pow).then_inc(s_rstd2, 1)

            def step(b, p):
                prev, cur, nxt, prep, norm = present(b)
                own.count = 0
                pool.sem_clear(s_pool)
                if norm:
                    normalise_x(b + 3, 1 - p)
                if prep:
                    variance(b + 2)
                    residual(b + 2)
                    third_part(b + 2)
                if isinstance(b, int) and NB - 2 <= b < NB:
                    scales(b - (NB - 2))

            def masks():
                own.count = 0
                pool.sem_clear(s_pool)
                pool.memset(head_mask[:], 1.0).then_inc(s_pool, 1)
                pool.wait_ge(s_pool, own.next())
                pool.affine_select(out=head_mask[:], in_=head_mask[:], compare_op=ALU.is_ge, fill=0.0,
                                   base=0, pattern=[[-D, H]], channel_multiplier=1).then_inc(s_pool, 1)
                pool.wait_ge(s_pool, own.next())
                pool.affine_select(out=head_mask[:], in_=head_mask[:], compare_op=ALU.is_ge, fill=0.0,
                                   base=D - 1, pattern=[[D, H]], channel_multiplier=-1).then_inc(s_pool, 1)
                pool.wait_ge(s_pool, own.next())
                pool.memset(seq_eye[:], 0.0).then_inc(s_pool, 1)
                pool.wait_ge(s_pool, own.next())
                pool.affine_select(out=seq_eye[:], in_=seq_eye[:], compare_op=ALU.not_equal, fill=1.0,
                                   base=0, pattern=[[0, QUAD], [-1, SEQ]], channel_multiplier=1).then_inc(s_pool, 1)
                pool.wait_ge(s_pool, own.next())
                pool.memset(causal[:], 0.0).then_inc(s_pool, 1)
                pool.wait_ge(s_pool, own.next())
                pool.affine_select(out=causal[:], in_=causal[:], compare_op=ALU.is_ge, fill=MASKED,
                                   base=0, pattern=[[0, H], [-1, SEQ]], channel_multiplier=1).then_inc(s_pool, 1)
                pool.wait_ge(s_pool, own.next())
                for e in range(NE):
                    ins = pool.memset(index8[:, :, e:e + 1], float(e))
                ins.then_inc(s_ident, 1)
                pool.memset(ones[:], 1.0).then_inc(s_pool, 1)
                pool.wait_ge(s_pool, own.next())
                pool.memset(Vexp[:], 0.0).then_inc(s_pool, 1)
                pool.wait_ge(s_pool, own.next())
                for q in range(QUAD):
                    pool.memset(Vexp[q * SEQ:(q + 1) * SEQ, :, :, q, D:D + 1], 1.0).then_inc(s_vones, 1)
                    pool.wait_ge(s_vones, q + 1)

            run_steps(pool, step, {-2: masks})

            def sum_xz(n, p):
                pool.wait_ge(s_xg[p], n * 32 + (64 - 32 * p))
                pool.wait_ge(s_zg[p], n * 32 + (64 - 32 * p))
                if positive(n - 1):
                    pool.wait_ge(s_acc0, n - 1)
                pool.tensor_tensor(xzg[p][:], xg[p][:], zg[p][:], ALU.add).then_inc(s_xzg, 1)

            def step(g, p):
                ffn, tail, head, norm = group_present(g)
                own.count = 0
                pool.sem_clear(s_pool)
                if tail:
                    sum_xz(g + 1, 1 - p)
                    scales2(g + 1)
                if norm:
                    scales(g + 3)

            run_groups(pool, step)

        @block.tensor
        def _(pe):
            pe.wait_ge(s_ident, 1)
            pe.wait_ge(s_setup, 1)
            pe.wait_ge(s_dma_w, 64)

            def mm(o, l, r, start=True, stop=True):
                return pe.matmul(o, l, r, start=start, stop=stop, skip_group_check=True)

            def misc16(m):
                return misc[m][:].bitcast(BF16)

            def xn_transposes(n, p):
                pe.wait_ge(s_xn, n + 1)
                for st in range(ST):
                    ins = pe.transpose(misc[1][:, st * P:(st + 1) * P], xn[:, st, :], ident[:])
                ins.then_inc(s_xt_ps, 1)

            def project_qk(n, p):
                pe.wait_ge(s_xt, n + 1)
                for st in range(ST):
                    ins = mm(misc[1][:, st * 256:(st + 1) * 256], xnT[p][:, st * P:(st + 1) * P],
                             wqk[:].rearrange("p a h d -> p (a h d)"))
                ins.then_inc(s_qk_ps, 1)

            def project_v(n, p):
                for st in range(ST):
                    ins = mm(misc[1][:, st * P:(st + 1) * P], xnT[p][:, st * P:(st + 1) * P], wv[:])
                ins.then_inc(s_v_ps, 1)

            def stack_transposes(n, a, k):
                m = misc16(1 if (a == 1 and k == 0) else 0)
                if k == 0:
                    pe.wait_ge(s_stack, 2 * (n + 1))
                    pe.wait_ge(s_third, n + 1)
                for q in range(HP):
                    for st in range(ST):
                        h = 2 * (HP * k + q)
                        ins = pe.transpose(m[:, q * NS + st * P:q * NS + (st + 1) * P],
                                           stack[:, a, st, h:h + 2, :].rearrange("p h k -> p (h k)"), identb[:])
                ins.then_inc((s_qt_ps if a == 0 else s_kt_ps)[k], 1)

            def row_pass(n, p, h):
                if h % 8 == 0:
                    pe.wait_ge(s_qt[h // 8], n + 1)
                    pe.wait_ge(s_kt[h // 8], n + 1)
                if h == 0:
                    if positive(H * n):
                        pe.wait_ge(s_max, H * n)
                elif h >= 3:
                    pe.wait_ge(s_max, H * n + h - 2)
                q = h // 2
                for st in range(ST):
                    ins = mm(row_scores[h % 3][:, st * NS:(st + 1) * NS],
                             QT[p][:, q, st * P:(st + 1) * P], KT[p][h % 2][:, q, :])
                ins.then_inc(s_row, 1)

            def col_pass(b, p, h):
                if h % 8 == 0:
                    pe.wait_ge(s_shd[h // 8], 64 * (b + 1))
                if positive(H * b + h - 1):
                    pe.wait_ge(s_exp, H * b + h - 1)
                q = h // 2
                for tc in range(ST):
                    ins = mm(col_scores[h % 2][:, tc * NS:(tc + 1) * NS],
                             KT[p][h % 2][:, q, tc * P:(tc + 1) * P], QT[p][:, q, :])
                ins.then_inc(s_col, 1)

            def pv(b, p, g, tc):
                if tc == 0:
                    pe.wait_ge(s_exp, H * b + 4 * g + 4)
                    if g == 0 and positive(b):
                        pe.wait_ge(s_ot[1], b)
                    if g == 2:
                        pe.wait_ge(s_ot[0], b + 1)
                for j in range(4):
                    h = 4 * g + j
                    ins = mm(pv_bank[32 * j:32 * j + FEAT, (g % 2) * NS:(g % 2 + 1) * NS],
                             V[p][:, tc, h, :], prob[:, h % 8, tc, :],
                             start=(tc == 0), stop=(tc == ST - 1))
                if tc == ST - 1:
                    ins.then_inc(s_pv, 1)

            def out_transposes(b, k):
                pe.wait_ge(s_ot[k], b + 1)
                for g in range(2):
                    for st in range(ST):
                        c = (g * ST + st) * P
                        ins = pe.transpose(misc[0][:, c:c + P], oT[k][:, g, st * P:(st + 1) * P], ident[:])
                ins.then_inc(s_on_ps[k], 1)

            def merge_transposes(b):
                pe.wait_ge(s_on[1], b + 1)
                for st in range(ST):
                    ins = pe.transpose(misc[0][:, st * P:(st + 1) * P],
                                       o_nat[:, st].rearrange("p h d -> p (h d)"), ident[:])
                ins.then_inc(s_oa_ps, 1)

            def project_out(b):
                pe.wait_ge(s_oa, b + 1)
                for st in range(ST):
                    ins = mm(misc[0][:, st * P:(st + 1) * P], oT_all[:, st * P:(st + 1) * P], wo[:])
                ins.then_inc(s_pr_ps, 1)

            def shift_transposes(n, k):
                pe.wait_ge(s_shift[k], n + 1)
                for st in range(ST):
                    ins = pe.transpose(misc16(1)[0:SROWS, st * P:(st + 1) * P],
                                       shift[k][:, st].rearrange("p a r q -> p (a r q)"), identb[:])
                ins.then_inc(s_sht_ps[k], 1)

            def hn_transposes(n):
                pe.wait_ge(s_gxh, n + 1)
                if isinstance(n, int) and n == 0:
                    pe.wait_ge(s_max, H * NB)
                    pe.wait_ge(s_setup, 4)
                if positive(n):
                    pe.wait_ge(s_vexp, n)
                for t in range(TILES):
                    ins = pe.transpose(head_bank(n)[:, t * P:(t + 1) * P], gxh[:, t, :], ident[:])
                ins.then_inc(s_hn_ps, 1)

            def causal_q(n):
                pe.wait_ge(s_hn, n + 1)
                mm(head_bank(n)[:], in_wT[:, 0:E], hnT[:]).then_inc(s_gq_ps, 1)

            def causal_k(n):
                pe.wait_ge(s_gq, n + 1)
                mm(head_bank(n)[:], in_wT[:, E:2 * E], hnT[:]).then_inc(s_gk_ps, 1)

            def causal_v(n):
                pe.wait_ge(s_kexp, n + 1)
                for t in range(TILES):
                    ins = mm(head_bank(n)[:, t * P:(t + 1) * P], hnT[:, t * P:(t + 1) * P], in_wT[:, 2 * E:3 * E])
                ins.then_inc(s_gv_ps, 1)

            def causal_scores(n, t):
                if t < 2:
                    if positive(2 * (n - 1) + t + 1):
                        pe.wait_ge(s_son, 2 * (n - 1) + t + 1)
                else:
                    pe.wait_ge(s_sdiff, 4 * n + t - 1)
                m = score_bank(n, t)
                mm(m[:], seq_eye[:].rearrange("k n s -> k (n s)"), causal[:].rearrange("k h t -> k (h t)"),
                   stop=False)
                for q in range(QUAD):
                    c = t * P + q * SEQ
                    ins = mm(m[q * SEQ:(q + 1) * SEQ, :], gqT[:, c:c + SEQ],
                             Kexp[:, t * QUAD + q].rearrange("p h t -> p (h t)"), start=False)
                ins.then_inc(s_sc, 1)

            def step(b, p):
                prev, cur, nxt, prep, norm = present(b)
                for h in range(H):
                    if cur:
                        col_pass(b, p, h)
                    for tc in range(ST):
                        if h == tc and prev:
                            pv(b - 1, 1 - p, 3, tc)
                        if h % 4 == 1 + tc and h > 4 and cur:
                            pv(b, p, h // 4 - 1, tc)
                    if h == PE_AT["q1"] and nxt:
                        if prev:
                            pe.wait_ge(s_on[0], b)
                        else:
                            pe.wait_ge(s_qt[0], b + 2)
                        stack_transposes(b + 1, 0, 1)
                    if nxt:
                        row_pass(b + 1, 1 - p, h)
                    if h == PE_AT["k1"] and nxt:
                        pe.wait_ge(s_qt[1], b + 2)
                        stack_transposes(b + 1, 1, 1)
                    if h == PE_AT["out1"] and prev:
                        if nxt:
                            pe.wait_ge(s_kt[1], b + 2)
                        else:
                            pe.wait_ge(s_on[0], b)
                        out_transposes(b - 1, 1)
                    if h == PE_AT["merge"] and prev:
                        merge_transposes(b - 1)
                    if h == PE_AT["project"] and prev:
                        project_out(b - 1)
                    if h == PE_AT["q0"] and prep:
                        if prev:
                            pe.wait_ge(s_z, b)
                        elif nxt:
                            pe.wait_ge(s_kt[1], b + 2)
                        stack_transposes(b + 2, 0, 0)
                    if h == PE_AT["out0"] and cur:
                        if prep:
                            pe.wait_ge(s_qt[0], b + 3)
                        else:
                            pe.wait_ge(s_z, b)
                        out_transposes(b, 0)
                    if h == PE_AT["shift1"] and cur:
                        if prep:
                            pe.wait_ge(s_feat, 2 * (b + 3))
                        elif nxt:
                            pe.wait_ge(s_kt[0], b + 2)
                        else:
                            pe.wait_ge(s_sht[0], b + 1)
                        shift_transposes(b, 1)
                    if h == PE_AT["v"] and nxt:
                        if cur:
                            pe.wait_ge(s_sht[1], b + 1)
                        else:
                            pe.wait_ge(s_feat, 2 * (b + 3))
                        project_v(b + 1, 1 - p)
                    if h == PE_AT["x"] and norm:
                        if nxt:
                            pe.wait_ge(s_v, b + 2)
                        elif prep:
                            pe.wait_ge(s_feat, 2 * (b + 3))
                        xn_transposes(b + 3, 1 - p)
                    if h == PE_AT["shift0"] and nxt:
                        if norm:
                            pe.wait_ge(s_xt, b + 4)
                        else:
                            pe.wait_ge(s_v, b + 2)
                        shift_transposes(b + 1, 0)
                    if h == PE_AT["k0"] and prep:
                        if nxt:
                            pe.wait_ge(s_sht[0], b + 2)
                        else:
                            pe.wait_ge(s_xt, b + 4)
                        stack_transposes(b + 2, 1, 0)
                    if h == PE_AT["qk"] and norm:
                        if prep:
                            pe.wait_ge(s_kt[0], b + 3)
                        project_qk(b + 3, 1 - p)
                    first_head(b, h)

            def first_head(b, h):
                slot = first_slot(b, h)
                if slot == PE_FIRST["hn"]:
                    hn_transposes(0)
                if slot == PE_FIRST["q"]:
                    causal_q(0)
                if slot == PE_FIRST["k"]:
                    causal_k(0)
                if slot == PE_FIRST["v"]:
                    causal_v(0)
                for t in range(TILES):
                    if slot == PE_FIRST[f"scores{t}"]:
                        causal_scores(0, t)

            def prepare():
                pe.wait_ge(s_zeroed, 1)
                pe.wait_ge(s_setup, 2)
                mm(row_scores[0][:, E:E + 1], ones[:], w1_max[:])
                mm(row_scores[0][:, 0:E], bv_wide[:], out_wT[:]).then_inc(s_bvw, 1)
                pe.wait_ge(s_setup, 3)

            run_steps(pe, step, {-1: prepare})

            pe.wait_ge(s_z, NB)

            def causal_pv(n):
                pe.wait_ge(s_spT, 4 * (n + 1))
                pe.wait_ge(s_vexp, n + 1)
                for h in range(H):
                    c = (h % 8) * QUAD * FEAT
                    for t in range(TILES):
                        ins = mm(seq_bank[h // 8][t * SEQ:(t + 1) * SEQ, c:c + QUAD * FEAT],
                                 sprobT[:, t, h, :], Vexp[:, t, h].rearrange("p n c -> p (n c)"))
                    if h % 8 == 7:
                        ins.then_inc(s_spv, 1)

            def merged_transposes(n):
                pe.wait_ge(s_son, 2 * (n + 1))
                if positive(n):
                    pe.wait_ge(s_ld, n)
                for q in range(QUAD):
                    ins = pe.transpose(misc[1][:, q * P:(q + 1) * P], so_nat[:, q].rearrange("p h d -> p (h d)"),
                                       ident[:])
                ins.then_inc(s_a_ps, 1)

            def causal_out(n):
                pe.wait_ge(s_a, n + 1)
                for t in range(TILES):
                    ins = mm(misc[1][:, t * P:(t + 1) * P], aT[:, t].rearrange("p n s -> p (n s)"), out_wT[:])
                ins.then_inc(s_pj_ps, 1)

            def h2_transposes(n):
                pe.wait_ge(s_h2n, n + 1)
                for t in range(TILES):
                    ins = pe.transpose(misc[1][:, t * P:(t + 1) * P], h2n[:, t, :], ident[:])
                ins.then_inc(s_h2_ps, 1)

            def router_logits(n):
                pe.wait_ge(s_h2, n + 1)
                for t in range(TILES):
                    ins = mm(misc[1][:, t * NE:(t + 1) * NE], hn2T[:, t * P:(t + 1) * P], router[:])
                ins.then_inc(s_lg_ps, 1)

            def expert_up(g, p, e, c):
                if e == 0 and c == 0:
                    pe.wait_ge(s_split, g + 1)
                if positive(NE * FC * g + FC * e + c - 1):
                    pe.wait_ge(s_mid, NE * FC * g + FC * e + c - 1)
                f = slice(c * P, (c + 1) * P)
                mm(up_bank[c][:], w1_lo[:, e, f], hn2_hi[p][:], stop=False)
                mm(up_bank[c][:], w1_hi[:, e, f], hn2_lo[p][:], start=False, stop=False)
                mm(up_bank[c][:], w1_hi[:, e, f], hn2_hi[p][:], start=False).then_inc(s_up, 1)

            def expert_down(g, e):
                pe.wait_ge(s_mid, NE * FC * g + FC * (e + 1))
                if positive(NE * g + e - 1):
                    pe.wait_ge(s_acc, NE * g + e - 1)
                for t in range(TILES):
                    for c in range(FC):
                        ins = mm(down_bank[e % 2][:, t * P:(t + 1) * P], hmid[e % 2][c][:, t * P:(t + 1) * P],
                                 w2_sb[:, e, c, :], start=(c == 0), stop=(c == FC - 1))
                ins.then_inc(s_dn, 1)

            def group_step(g, p):
                ffn, tail, head, norm = group_present(g)
                for u in range(FC * NE):
                    e, c = u // FC, u % FC
                    if ffn:
                        expert_up(g, p, e, c)
                    if u == PE_G["hn"] and head:
                        hn_transposes(g + 2)
                    if u == PE_G["q"] and head:
                        causal_q(g + 2)
                    if u == PE_G["k"] and head:
                        causal_k(g + 2)
                    if u == PE_G["v"] and head:
                        causal_v(g + 2)
                    if u == PE_G["pv"] and tail:
                        causal_pv(g + 1)
                    for t in range(TILES):
                        if u == PE_G[f"scores{t}"] and head:
                            causal_scores(g + 2, t)
                    if u == PE_G["merge"] and tail:
                        merged_transposes(g + 1)
                    if u == PE_G["out"] and tail:
                        causal_out(g + 1)
                    if u == PE_G["h2"] and tail:
                        h2_transposes(g + 1)
                    if u == PE_G["router"] and tail:
                        router_logits(g + 1)
                    if ffn and c == FC - 1 and e > 0:
                        expert_down(g, e - 1)
                if ffn:
                    expert_down(g, NE - 1)

            run_groups(pe, group_step)

        @block.vector
        def _(dve):
            own = Own()
            dve.wait_ge(s_dma_w, 64)
            dve.tensor_reduce(wqk_mean[:], wqk_raw[:].rearrange("p a h d -> p (a h) d"), AX.X, ALU.add).then_inc(s_dve, 1)
            dve.wait_ge(s_dve, own.next())
            dve.tensor_scalar(wqk_mean[:], wqk_mean[:], 1.0 / D, None, ALU.mult).then_inc(s_dve, 1)
            dve.wait_ge(s_dve, own.next())
            dve.tensor_tensor(wqk[:].rearrange("p a h d -> p (a h) d"),
                              wqk_raw[:].rearrange("p a h d -> p (a h) d"),
                              wqk_mean[:].unsqueeze(2).broadcast_to([P, 2 * H, D]),
                              ALU.subtract).then_inc(s_setup, 1)

            def x_statistics(n, p):
                dve.wait_ge(s_x[p], n * 8 + (16 - 8 * p))
                if positive(n):
                    dve.wait_ge(s_xn, n)
                for st in range(ST):
                    ins = dve.bn_stats(stats[:, st, :], x_in[p][:, st, :])
                ins.then_inc(s_dve, 1)
                dve.wait_ge(s_dve, own.next())
                for st in range(ST):
                    ins = dve.bn_aggr(mv[:, st, :], stats[:, st, :])
                ins.then_inc(s_var, 1)

            def first_part(n):
                dve.wait_ge(s_ninth, n + 1)
                if positive(n):
                    dve.wait_ge(s_kt_ps[1], n)
                dve.tensor_copy(parts[:, :, 0:FEAT], feat[:].rearrange(flat)).then_inc(s_first, 1)

            def second_part(n):
                dve.wait_ge(s_resid, n + 1)
                dve.tensor_copy(parts[:, :, FEAT:2 * FEAT], resid[:].rearrange(flat)).then_inc(s_second, 1)

            def repeat_first(n):
                dve.wait_ge(s_first, n + 1)
                for a, place in ((0, 3), (1, 4)):
                    ins = dve.tensor_copy(slots[:, a, :, place:place + 3:2, :],
                                          slots[:, a, :, 0:1, :].broadcast_to([P, ST * H, 2, FEAT]))
                ins.then_inc(s_stack, 1)

            def repeat_second(n):
                dve.wait_ge(s_second, n + 1)
                for a, place in ((0, 4), (1, 3)):
                    ins = dve.tensor_copy(slots[:, a, :, place, :], slots[:, a, :, 1, :])
                ins.then_inc(s_stack, 1)

            def q_out(n, p, k):
                dve.wait_ge(s_qt_ps[k], n + 1)
                if positive(H * (n - 2) + 8 * k + 8):
                    dve.wait_ge(s_col, H * (n - 2) + 8 * k + 8)
                dve.tensor_copy(QT[p][:, HP * k:HP * (k + 1), :],
                                misc[0][:].bitcast(BF16).rearrange("p (q s) -> p q s", q=HP)).then_inc(s_qt[k], 1)

            def take_max(n, h):
                dve.wait_ge(s_row, H * n + h + 1)
                if h % 8 == 0:
                    if positive(n):
                        dve.wait_ge(s_shift[h // 8], n)
                dve.tensor_reduce(rowmax[h // 8][:, :, h % 2, h % 8 // 2],
                                  row_scores[h % 3][:].rearrange("p (s t) -> p s t", s=ST),
                                  AX.X, ALU.max).then_inc(s_max, 1)

            def negate(n, k):
                dve.wait_ge(s_max, H * n + 8 * k + 8)
                if positive(n):
                    dve.wait_ge(s_sht_ps[k], n)
                dve.tensor_scalar(shift[k][:, :, :, 0, :], rowmax[k][:], -1.0, None, ALU.mult).then_inc(s_dve, 1)
                dve.wait_ge(s_dve, own.next())
                dve.scalar_tensor_tensor(out=shift[k][:, :, :, 1, :], in0=rowmax[k][:], scalar=-1.0,
                                         in1=shift[k][:, :, :, 0, :],
                                         op0=ALU.mult, op1=ALU.subtract).then_inc(s_shift[k], 1)

            def normalise_out(b, k):
                dve.wait_ge(s_on_ps[k], b + 1)
                src = misc[0][:].rearrange("p (g s j c) -> p g s j c", g=2, s=ST, j=4)
                dve.reciprocal(rsum[k][:], src[:, :, :, :, D]).then_inc(s_dve, 1)
                dve.wait_ge(s_dve, own.next())
                if positive(b):
                    dve.wait_ge(s_oa_ps, b)
                for g in range(2):
                    ins = dve.tensor_tensor(o_nat[:, :, 8 * k + 4 * g:8 * k + 4 * g + 4, :],
                                            src[:, g, :, :, 0:D],
                                            rsum[k][:, g].unsqueeze(3).broadcast_to([P, ST, 4, D]), ALU.mult)
                ins.then_inc(s_on[k], 1)

            def group_statistics(n, p):
                dve.wait_ge(s_xg[p], n * 32 + (64 - 32 * p))
                if positive(n):
                    dve.wait_ge(s_gxb, n)
                for t in range(TILES):
                    ins = dve.bn_stats(gstats[:, t, :], xg[p][:, t, :])
                ins.then_inc(s_dve, 1)
                dve.wait_ge(s_dve, own.next())
                for t in range(TILES):
                    ins = dve.bn_aggr(gmv[:, t, :], gstats[:, t, :])
                ins.then_inc(s_gvar, 1)

            def group_normalise(n, p):
                dve.wait_ge(s_gr, n + 1)
                if positive(n):
                    dve.wait_ge(s_hn_ps, n)
                for t in range(TILES):
                    ins = dve.tensor_scalar(gxh[:, t, :], xg[p][:, t, :], gmv[:, t, 0:1], gr12[:, t:t + 1],
                                            ALU.subtract, ALU.mult)
                ins.then_inc(s_gxh, 1)
                if positive(n - 1):
                    dve.wait_ge(s_xattn, n - 1)
                for t in range(TILES):
                    ins = dve.tensor_scalar(gxb[p][:, t, :], xg[p][:, t, :], gmv[:, t, 0:1], gr1[:, t:t + 1],
                                            ALU.subtract, ALU.mult)
                ins.then_inc(s_dve, 1)
                dve.wait_ge(s_dve, own.next())
                dve.tensor_tensor(gxb[p][:], gxb[p][:], ob_row[:].unsqueeze(1).broadcast_to([P, TILES, E]),
                                  ALU.add).then_inc(s_gxb, 1)

            def take_q(n):
                dve.wait_ge(s_gq_ps, n + 1)
                if positive(4 * n):
                    dve.wait_ge(s_sc, 4 * n)
                dve.tensor_scalar(gqT[:], head_bank(n)[:], in_bT[:, 0:1], None, ALU.add).then_inc(s_gq, 1)

            def take_v(n):
                dve.wait_ge(s_gv_ps, n + 1)
                if positive(2 * n):
                    dve.wait_ge(s_spv, 2 * n)
                ps = head_bank(n)[:].rearrange("p (t h d) -> p t h d", t=TILES, h=H)
                for q in range(QUAD):
                    rows = slice(q * SEQ, (q + 1) * SEQ)
                    ins = dve.tensor_copy(Vexp[rows, :, :, q, 0:D], ps[rows])
                ins.then_inc(s_vexp, 1)

            def score_maxima(n, t):
                if isinstance(n, int) and n == 0 and t == 0:
                    dve.wait_ge(s_pv, 4 * NB)
                ps = score_bank(n, t)[:].rearrange("p (h t) -> p h t", h=H)
                dve.wait_ge(s_sc, 4 * n + t + 1)
                dve.tensor_reduce(smax[:, t, :], ps, AX.X, ALU.max).then_inc(s_dve, 1)
                dve.wait_ge(s_dve, own.next())
                if positive(4 * (n - 1) + t + 1):
                    dve.wait_ge(s_sprob, 4 * (n - 1) + t + 1)
                dve.tensor_tensor(sdiff[:, t], ps, smax[:, t, :].unsqueeze(2).broadcast_to([P, H, SEQ]),
                                  ALU.subtract).then_inc(s_sdiff, 1)

            def step(b, p):
                prev, cur, nxt, prep, norm = present(b)
                own.count = 0
                dve.sem_clear(s_dve)
                for h in range(H):
                    if h == DVE_AT["q1"] and nxt:
                        q_out(b + 1, 1 - p, 1)
                    if nxt:
                        take_max(b + 1, h)
                    if h == DVE_AT["statistics"] and norm:
                        x_statistics(b + 3, 1 - p)
                    if h == DVE_AT["first"] and prep:
                        first_part(b + 2)
                    if h == DVE_AT["out1"] and prev:
                        normalise_out(b - 1, 1)
                    if h == DVE_AT["second"] and prep:
                        second_part(b + 2)
                    if h == DVE_AT["shift0"] and nxt:
                        negate(b + 1, 0)
                    if h == DVE_AT["repeat1"] and prep:
                        repeat_first(b + 2)
                    if h == DVE_AT["repeat2"] and prep:
                        repeat_second(b + 2)
                    if h == DVE_AT["q0"] and prep:
                        q_out(b + 2, p, 0)
                    if h == DVE_AT["out0"] and cur:
                        normalise_out(b, 0)
                    first_head(b, h)
                if nxt:
                    negate(b + 1, 1)

            def first_head(b, h):
                slot = first_slot(b, h)
                for n in range(2):
                    if slot == DVE_FIRST[f"statistics{n}"]:
                        group_statistics(n, n)
                    if slot == DVE_FIRST[f"normalise{n}"]:
                        group_normalise(n, n)
                if slot == DVE_FIRST["q"]:
                    take_q(0)
                if slot == DVE_FIRST["v"]:
                    take_v(0)
                for t in range(TILES):
                    if slot == DVE_FIRST[f"max{t}"]:
                        score_maxima(0, t)

            def zero():
                own.count = 0
                dve.sem_clear(s_dve)
                for t in (*KT[0], *KT[1], stack):
                    dve.memzero(t[:]).then_inc(s_dve, 1)
                    dve.wait_ge(s_dve, own.next())
                for t in V:
                    dve.memset(t[:], 1.0).then_inc(s_dve, 1)
                    dve.wait_ge(s_dve, own.next())
                dve.memset(pv_bank[:], 0.0).then_inc(s_dve, 1)
                dve.wait_ge(s_dve, own.next())
                dve.memset(stack[:, 1, :, :, SHIFT:SHIFT + SPARTS], 1.0).then_inc(s_zeroed, 1)
                dve.wait_ge(s_zeroed, 1)

            def prepare():
                dve.wait_ge(s_ident, 2)
                dve.wait_ge(s_vones, QUAD)
                dve.wait_ge(s_dma_w2, 16 * 11)
                own.count = 0
                dve.sem_clear(s_dve)
                dve.tensor_copy(bv_wide[:], in_bT[:, 2:3].broadcast_to([P, P]))
                dve.tensor_scalar(head_bias[:], head_mask[:], in_bT[:, 1:2], None, ALU.mult)
                dve.tensor_scalar(hn2_scale[:], ln2w[:], -1.0, None, ALU.mult)
                dve.tensor_scalar(up_scale[:], ln2b[:], -1.0, None, ALU.mult).then_inc(s_dve, 1)
                dve.wait_ge(s_dve, own.next())
                dve.tensor_tensor(hn2_scale[:], hn2_scale[:], ln2w[:], ALU.max)
                dve.tensor_tensor(up_scale[:], up_scale[:], ln2b[:], ALU.max).then_inc(s_dve, 1)
                dve.wait_ge(s_dve, own.next())
                dve.tensor_scalar(hn2_scale[:], hn2_scale[:], 12.0, 1.0e-30, ALU.mult, ALU.add).then_inc(s_dve, 1)
                dve.wait_ge(s_dve, own.next())
                dve.tensor_tensor(bound[:], hn2_scale[:], up_scale[:], ALU.add).then_inc(s_dve, 1)
                dve.wait_ge(s_dve, own.next())
                dve.reciprocal(hn2_scale[:], bound[:]).then_inc(s_dve, 1)
                dve.tensor_scalar(w1_sb[:], w1_sb[:], bound[:, 0:1], None, ALU.mult).then_inc(s_dve, 1)
                own.next()
                dve.wait_ge(s_dve, own.next())
                dve.tensor_scalar(hn2_scale[:], hn2_scale[:], HN2_TOP, None, ALU.mult)
                dve.tensor_reduce(w1_max[:], w1_sb[:].rearrange("p e f -> p (e f)"), AX.X, ALU.max)
                dve.tensor_reduce(w1_scale[:], w1_sb[:].rearrange("p e f -> p (e f)"), AX.X, ALU.min).then_inc(s_dve, 1)
                dve.wait_ge(s_dve, own.next())
                dve.tensor_scalar(w1_scale[:], w1_scale[:], -1.0, None, ALU.mult).then_inc(s_dve, 1)
                dve.wait_ge(s_dve, own.next())
                dve.tensor_tensor(w1_max[:], w1_max[:], w1_scale[:], ALU.max).then_inc(s_setup, 1)
                dve.wait_ge(s_bvw, 1)
                dve.tensor_tensor(ob_row[:], row_scores[0][:, 0:E], ob_raw[:], ALU.add)
                dve.tensor_scalar(w1_sum[:], row_scores[0][:, E:E + 1], 1.0e-30, None, ALU.add).then_inc(s_setup, 1)
                dve.wait_ge(s_setup, 3)
                dve.tensor_scalar(up_scale[:], w1_sum[:], 1.0 / (HN2_TOP * W1_TOP), None, ALU.mult)
                dve.reciprocal(w1_scale[:], w1_sum[:]).then_inc(s_dve, 1)
                dve.wait_ge(s_dve, own.next())
                dve.tensor_scalar(w1_scale[:], w1_scale[:], W1_TOP, None, ALU.mult).then_inc(s_dve, 1)
                dve.wait_ge(s_dve, own.next())
                dve.tensor_scalar(w1_hi[:], w1_sb[:], w1_scale[:, 0:1], None, ALU.mult).then_inc(s_dve, 1)
                dve.wait_ge(s_dve, own.next())
                dve.scalar_tensor_tensor(out=w1_lo[:], in0=w1_sb[:], scalar=w1_scale[:, 0:1], in1=w1_hi[:],
                                         op0=ALU.mult, op1=ALU.subtract).then_inc(s_setup, 1)

            run_steps(dve, step, {-2: zero, -1: prepare})

            def split_hn2(n, p):
                dve.wait_ge(s_h2, n + 1)
                if positive(NE * FC * (n - 1)):
                    dve.wait_ge(s_up, NE * FC * (n - 1))
                dve.tensor_scalar(hn2_hi[p][:], hn2T[:], hn2_scale[:, 0:1], None, ALU.mult).then_inc(s_dve, 1)
                dve.wait_ge(s_dve, own.next())
                dve.scalar_tensor_tensor(out=hn2_lo[p][:], in0=hn2T[:], scalar=hn2_scale[:, 0:1], in1=hn2_hi[p][:],
                                         op0=ALU.mult, op1=ALU.subtract).then_inc(s_split, 1)

            def block_transposes(n):
                if positive(2 * n):
                    dve.wait_ge(s_spv, 2 * n)
                for t in range(TILES):
                    dve.wait_ge(s_sprob, 4 * n + t + 1)
                    dve.transpose(sprobT[:, t].rearrange("p h s -> p (h s)"),
                                  sprob[:, t].rearrange("p h s -> p (h s)")).then_inc(s_spT, 1)

            def causal_normalise(n):
                for k in range(2):
                    dve.wait_ge(s_spv, 2 * n + k + 1)
                    src = seq_bank[k][:, 0:8 * QUAD * FEAT].rearrange("p (h n c) -> p h n c", h=8, n=QUAD)
                    dve.reciprocal(srec[k][:], src[:, :, :, D]).then_inc(s_dve, 1)
                    dve.wait_ge(s_dve, own.next())
                    if positive(n):
                        dve.wait_ge(s_a_ps, n)
                    for q in range(QUAD):
                        ins = dve.tensor_tensor(so_nat[:, q, 8 * k:8 * k + 8, :], src[:, :, q, 0:D],
                                                srec[k][:, :, q].unsqueeze(2).broadcast_to([P, 8, D]), ALU.mult)
                    ins.then_inc(s_son, 1)

            def make_x1(n, p):
                dve.wait_ge(s_pj_ps, n + 1)
                if positive(n):
                    dve.wait_ge(s_h2n, n)
                dve.tensor_tensor(x1[:], misc[1][:].rearrange("p (t e) -> p t e", t=TILES), gxb[p][:],
                                  ALU.add).then_inc(s_xattn, 1)
                dve.wait_ge(s_xattn, n + 1)
                for t in range(TILES):
                    ins = dve.bn_stats(stats2[:, t, :], x1[:, t, :])
                ins.then_inc(s_dve, 1)
                dve.wait_ge(s_dve, own.next())
                for t in range(TILES):
                    ins = dve.bn_aggr(mv2[:, t, :], stats2[:, t, :])
                ins.then_inc(s_var2, 1)
                dve.wait_ge(s_xzg, n + 1)
                if positive(n * 32 - 32 * p):
                    dve.wait_ge(s_out[p], n * 32 - 32 * p)
                dve.tensor_tensor(acc[p][:], x1[:], xzg[p][:], ALU.add).then_inc(s_acc0, 1)

            def normalise_x1(n):
                dve.wait_ge(s_rstd2, n + 1)
                if positive(n):
                    dve.wait_ge(s_h2_ps, n)
                for t in range(TILES):
                    ins = dve.tensor_scalar(h2n[:, t, :], x1[:, t, :], mv2[:, t, 0:1], rstd2[:, t:t + 1],
                                            ALU.subtract, ALU.mult)
                ins.then_inc(s_h2n, 1)

            def choose(n):
                dve.wait_ge(s_lg_ps, n + 1)
                dve.tensor_copy(logit[:].rearrange("p t e -> p (t e)"), misc[1][:, 0:TILES * NE]).then_inc(s_dve, 1)
                dve.wait_ge(s_dve, own.next())
                for t in range(TILES):
                    ins = dve.max(top[:, t, :], logit[:, t, :])
                ins.then_inc(s_dve, 1)
                dve.wait_ge(s_dve, own.next())
                if positive(n):
                    dve.wait_ge(s_le, n)
                dve.tensor_tensor(ldiff[:], logit[:], top[:, :, 0:1].broadcast_to([P, TILES, NE]),
                                  ALU.subtract).then_inc(s_ld, 1)
                for t in range(TILES):
                    ins = dve.max_index(topi[:, t, :], top[:, t, :], logit[:, t, :])
                ins.then_inc(s_dve, 1)
                dve.wait_ge(s_dve, own.next())
                dve.tensor_copy(topf[:], topi[:, :, 0:2]).then_inc(s_dve, 1)
                dve.wait_ge(s_dve, own.next())
                for k in range(2):
                    ins = dve.tensor_tensor(pick[:, k], index8[:], topf[:, :, k:k + 1].broadcast_to([P, TILES, NE]),
                                            ALU.is_equal)
                ins.then_inc(s_dve, 1)
                dve.wait_ge(s_dve, own.next())
                dve.tensor_tensor(pick[:, 0], pick[:, 0], pick[:, 1], ALU.add).then_inc(s_dve, 1)
                dve.wait_ge(s_dve, own.next())

            def make_gates(n, p):
                dve.wait_ge(s_le, n + 1)
                dve.tensor_reduce(lsum[:], lexp[:], AX.X, ALU.add).then_inc(s_dve, 1)
                dve.wait_ge(s_dve, own.next())
                dve.reciprocal(lsum[:], lsum[:]).then_inc(s_dve, 1)
                dve.wait_ge(s_dve, own.next())
                dve.tensor_tensor(gate[p][:], lexp[:], pick[:, 0], ALU.mult).then_inc(s_dve, 1)
                dve.wait_ge(s_dve, own.next())
                dve.tensor_tensor(gate[p][:], gate[p][:], lsum[:].unsqueeze(2).broadcast_to([P, TILES, NE]),
                                  ALU.mult).then_inc(s_gate, 1)

            def add_expert(g, p, e):
                if e == 0:
                    dve.wait_ge(s_gate, g + 1)
                    dve.wait_ge(s_acc0, g + 1)
                dve.wait_ge(s_dn, NE * g + e + 1)
                if positive(NE * g + e):
                    dve.wait_ge(s_acc, NE * g + e)
                for t in range(TILES):
                    ins = dve.scalar_tensor_tensor(out=acc[p][:, t, :], in0=down_bank[e % 2][:, t * P:(t + 1) * P],
                                                   scalar=gate[p][:, t, e:e + 1], in1=acc[p][:, t, :],
                                                   op0=ALU.mult, op1=ALU.add)
                ins.then_inc(s_acc, 1)

            def group_step(g, p):
                ffn, tail, head, norm = group_present(g)
                own.count = 0
                dve.sem_clear(s_dve)
                for u in range(FC * NE):
                    e, c = u // FC, u % FC
                    if ffn and c == 1 and e > 0:
                        add_expert(g, p, e - 1)
                    if u == DVE_G["spT"] and tail:
                        block_transposes(g + 1)
                    if u == DVE_G["q"] and head:
                        take_q(g + 2)
                    if u == DVE_G["seq_out"] and tail:
                        causal_normalise(g + 1)
                    if u == DVE_G["x1"] and tail:
                        make_x1(g + 1, 1 - p)
                    if u == DVE_G["h2"] and tail:
                        normalise_x1(g + 1)
                    if u == DVE_G["v"] and head:
                        take_v(g + 2)
                    if u == DVE_G["split"] and tail:
                        split_hn2(g + 1, 1 - p)
                    for t in range(TILES):
                        if u == DVE_G[f"max{t}"] and head:
                            score_maxima(g + 2, t)
                    if u == DVE_G["choose"] and tail:
                        choose(g + 1)
                    if u == DVE_G["statistics"] and norm:
                        group_statistics(g + 3, 1 - p)
                    if u == DVE_G["normalise"] and norm:
                        group_normalise(g + 3, 1 - p)
                if tail:
                    make_gates(g + 1, 1 - p)
                if ffn:
                    add_expert(g, p, NE - 1)

            run_groups(dve, group_step)

        @block.scalar
        def _(act):
            def copy_out(b, k):
                act.wait_ge(s_pv, 4 * b + 2 * k + 2)
                if positive(b):
                    act.wait_ge(s_on_ps[k], b)
                act.copy(oT[k][:].rearrange("p g s -> p (g s)"), pv_bank[:]).then_inc(s_ot[k], 1)

            def x_out(n, p):
                act.wait_ge(s_xt_ps, n + 1)
                if positive(n - 1):
                    act.wait_ge(s_v_ps, n - 1)
                act.copy(xnT[p][:], misc[1][:, 0:NS]).then_inc(s_xt, 1)

            def features(n):
                act.wait_ge(s_qk_ps, n + 1)
                if positive(n):
                    act.wait_ge(s_resid, n)
                ps = misc[1][:].rearrange("p (s a h d) -> p a s h d", s=ST, a=2, h=H)
                for a in range(2):
                    ins = act.copy(feat[:, a, :, 0:D].rearrange("p (s h) d -> p s h d", s=ST), ps[:, a])
                ins.then_inc(s_feat, 1)
                for a in range(2):
                    ins = act.activation(sq[:, a].rearrange("p (s h) d -> p s h d", s=ST), ps[:, a], ACT.Square,
                                         scale=(D - 1) ** -0.5)
                ins.then_inc(s_feat, 1)

            def merged_out(b):
                act.wait_ge(s_oa_ps, b + 1)
                if positive(b):
                    act.wait_ge(s_pr_ps, b)
                act.copy(oT_all[:], misc[0][:, 0:NS]).then_inc(s_oa, 1)

            def take_output(b, p):
                act.wait_ge(s_pr_ps, b + 1)
                if positive(b * 8 - 8 * p):
                    act.wait_ge(s_zd[p], b * 8 - 8 * p)
                act.copy(z_out[p][:].rearrange("p s e -> p (s e)"), misc[0][:, 0:NS]).then_inc(s_z, 1)

            def v_out(n, p):
                act.wait_ge(s_v_ps, n + 1)
                if positive(4 * (n - 1)):
                    act.wait_ge(s_pv, 4 * (n - 1))
                act.copy(V[p][:, :, :, 0:D],
                         misc[1][:, 0:NS].rearrange("p (s h d) -> p s h d", s=ST, h=H)).then_inc(s_v, 1)

            def k_out(n, p, k, a):
                if isinstance(n, int) and n == 0:
                    act.wait_ge(s_zeroed, 1)
                if a == 0:
                    act.wait_ge(s_kt_ps[k], n + 1)
                    if positive(H * (n - 2) + 8 * k + 8):
                        act.wait_ge(s_col, H * (n - 2) + 8 * k + 8)
                ps = misc[1 - k][:].bitcast(BF16).rearrange("p (q s) -> p q s", q=HP)
                half = slice(HP * k, HP * (k + 1))
                rows = slice(a * STACK, (a + 1) * STACK)
                ins = act.copy(KT[p][a][rows, half, :], ps[rows])
                if a == 1:
                    ins.then_inc(s_kt[k], 1)

            def probabilities(b, h):
                act.wait_ge(s_col, H * b + h + 1)
                if h % 4 == 0:
                    if positive(4 * b + h // 4 - 1):
                        act.wait_ge(s_pv, 4 * b + h // 4 - 1)
                act.activation(prob[:, h % 8].rearrange("p t s -> p (t s)"), col_scores[h % 2][:], ACT.Exp,
                               scale=1.0 / D).then_inc(s_exp, 1)

            def shift_out(n, k):
                act.wait_ge(s_sht_ps[k], n + 1)
                if positive(64 * n):
                    act.wait_ge(s_shd[k], 64 * n)
                act.copy(shiftT[k][:], misc[1][:].bitcast(BF16)[0:SROWS, 0:NS]).then_inc(s_sht[k], 1)

            def hn_out(n):
                act.wait_ge(s_hn_ps, n + 1)
                if positive(n):
                    act.wait_ge(s_gv_ps, n)
                act.activation(hnT[:], head_bank(n)[:], ACT.Identity, bias=ln1b[:, 0:1],
                               scale=ln1w[:, 0:1]).then_inc(s_hn, 1)

            def expand_k(n, lo, hi):
                if lo == 0:
                    act.wait_ge(s_gk_ps, n + 1)
                    if positive(4 * n):
                        act.wait_ge(s_sc, 4 * n)
                for h in range(lo, hi):
                    ins = act.activation(Kexp[:, :, h, :], head_bank(n)[:].rearrange("p (n t) -> p n t", n=GPOS),
                                         ACT.Identity, bias=head_bias[:, h:h + 1], scale=head_mask[:, h:h + 1])
                if hi == H:
                    ins.then_inc(s_kexp, 1)

            def causal_exp(n, t):
                if isinstance(n, int) and n == 0 and t == 0:
                    act.wait_ge(s_pv, 4 * NB)
                act.wait_ge(s_sdiff, 4 * n + t + 1)
                if positive(4 * (n - 1) + t + 1):
                    act.wait_ge(s_spT, 4 * (n - 1) + t + 1)
                act.activation(sprob[:, t], sdiff[:, t], ACT.Exp, scale=float(D) ** -0.5).then_inc(s_sprob, 1)

            def step(b, p):
                prev, cur, nxt, prep, norm = present(b)
                for h in range(H):
                    if cur:
                        probabilities(b, h)
                    if h == ACT_AT["copy_out1"] and prev:
                        copy_out(b - 1, 1)
                    if h == ACT_AT["features"] and prep:
                        features(b + 2)
                    if h == ACT_AT["shift1"] and cur:
                        shift_out(b, 1)
                    if nxt:
                        for a in range(2):
                            if h == ACT_AT["k1"] + a:
                                k_out(b + 1, 1 - p, 1, a)
                    if h == ACT_AT["v"] and nxt:
                        v_out(b + 1, 1 - p)
                    if h == ACT_AT["x"] and norm:
                        x_out(b + 3, 1 - p)
                    if h == ACT_AT["merged"] and prev:
                        merged_out(b - 1)
                    if h == ACT_AT["shift0"] and nxt:
                        shift_out(b + 1, 0)
                    if h == ACT_AT["output"] and prev:
                        take_output(b - 1, 1 - p)
                    if h == ACT_AT["copy_out0"] and cur:
                        copy_out(b, 0)
                    if prep:
                        for a in range(2):
                            if h == ACT_AT["k0"] + a:
                                k_out(b + 2, p, 0, a)
                    first_head(b, h)

            def first_head(b, h):
                slot = first_slot(b, h)
                if slot == ACT_FIRST["hn"]:
                    act.wait_ge(s_setup, 4)
                    hn_out(0)
                for i in range(H // 2):
                    if slot == ACT_FIRST["k0"] + i:
                        expand_k(0, 2 * i, 2 * i + 2)
                for t in range(TILES):
                    if slot == ACT_FIRST[f"exp{t}"]:
                        causal_exp(0, t)

            run_steps(act, step)

            def merged_rows(n):
                act.wait_ge(s_a_ps, n + 1)
                if positive(n):
                    act.wait_ge(s_pj_ps, n)
                act.copy(aT[:], misc[1][:].rearrange("p (n t s) -> p t n s", n=QUAD, t=TILES)).then_inc(s_a, 1)

            def h2_out(n):
                act.wait_ge(s_h2_ps, n + 1)
                if positive(n):
                    act.wait_ge(s_split, n)
                    act.wait_ge(s_lg_ps, n)
                act.activation(hn2T[:], misc[1][:], ACT.Identity, bias=ln2b[:, 0:1],
                               scale=ln2w[:, 0:1]).then_inc(s_h2, 1)

            def router_exp(n):
                act.wait_ge(s_ld, n + 1)
                if positive(n):
                    act.wait_ge(s_gate, n)
                act.activation(lexp[:], ldiff[:], ACT.Exp).then_inc(s_le, 1)

            def hidden(g, e, c):
                act.wait_ge(s_up, NE * FC * g + FC * e + c + 1)
                if c == 0 and positive(NE * g + e - 1):
                    act.wait_ge(s_dn, NE * g + e - 1)
                act.activation(hmid[e % 2][c][:], up_bank[c][:], ACT.Gelu,
                               scale=up_scale[:, 0:1]).then_inc(s_mid, 1)

            def group_step(g, p):
                ffn, tail, head, norm = group_present(g)
                for u in range(FC * NE):
                    e, c = u // FC, u % FC
                    if ffn:
                        hidden(g, e, c)
                    if u == ACT_G["hn"] and head:
                        hn_out(g + 2)
                    if u == ACT_G["merged"] and tail:
                        merged_rows(g + 1)
                    if u == ACT_G["h2"] and tail:
                        h2_out(g + 1)
                    for i in range(H // 2):
                        if u == ACT_G[f"k{i}"] and head:
                            expand_k(g + 2, 2 * i, 2 * i + 2)
                if tail:
                    router_exp(g + 1)
                if head:
                    for t in range(TILES):
                        causal_exp(g + 2, t)

            run_groups(act, group_step)

        @block.sync
        def _(sp):
            def load_x(b, p):
                if positive(b - 1):
                    sp.wait_ge(s_xn, b - 1)
                sp.dma_start(x_in[p][:], x[b].rearrange("(s p) e -> p s e", p=P)).then_inc(s_x[p], 16)

            def place_shift(n, p, k):
                sp.wait_ge(s_sht[k], n + 1)
                for a in range(2):
                    for r in range(SPARTS):
                        row, src = STACK * a + SHIFT + r, (a * SPARTS + r) * HP
                        sp.dma_start(QT[p][row:row + 1, HP * k:HP * (k + 1), :],
                                     shiftT[k][src:src + HP, :]).then_inc(s_shd[k], 16)

            def store_z(b, p):
                sp.wait_ge(s_z, b + 1)
                sp.dma_start(z_dram[b].rearrange("(s p) e -> p s e", p=P), z_out[p][:]).then_inc(s_zd[p], 16)

            def rows(a, n, q):
                return a.rearrange("b (g t q) e -> g q b t e", t=TILES, q=QUAD)[n, q]

            def load_x_group(n, p):
                if positive(n - 1):
                    sp.wait_ge(s_gxb, n - 1)
                    sp.wait_ge(s_xzg, n - 1)
                for q in range(QUAD):
                    sp.dma_start(xg[p][q * SEQ:(q + 1) * SEQ], rows(x, n, q)).then_inc(s_xg[p], 16)

            def load_z_group(n, p):
                if positive(n - 1):
                    sp.wait_ge(s_xzg, n - 1)
                for q in range(QUAD):
                    sp.dma_start(zg[p][q * SEQ:(q + 1) * SEQ], rows(z_dram, n, q)).then_inc(s_zg[p], 16)

            def step(b, p):
                prev, cur, nxt, prep, norm = present(b)
                if cur:
                    place_shift(b, p, 1)
                if prev:
                    store_z(b - 1, 1 - p)
                if nxt:
                    place_shift(b + 1, 1 - p, 0)
                if norm and not (isinstance(b, int) and b + 4 >= NB):
                    load_x(b + 4, p)
                if isinstance(b, int) and NB - 3 <= b < NB - 1:
                    load_x_group(b - (NB - 3), (b - (NB - 3)) % 2)

            load_x(0, 0)
            for dst, src in ((wqk_raw[:, 0], Wq.rearrange("e (h d) -> e h d", h=H)),
                             (wqk_raw[:, 1], Wk.rearrange("e (h d) -> e h d", h=H)),
                             (wv[:], Wv), (wo[:], Wo)):
                sp.dma_start(dst, src).then_inc(s_dma_w, 16)
            for dst, src in ((in_wT[:], in_w_t), (in_bT[:], in_b.rearrange("(c p) -> p c", p=P)),
                             (out_wT[:], out_w_t), (ob_raw[:], out_b.rearrange("(a e) -> a e", a=1).broadcast_to([P, E])),
                             (ln1w[:], ln1_w.rearrange("(p a) -> p a", a=1)),
                             (ln1b[:], ln1_b.rearrange("(p a) -> p a", a=1)),
                             (ln2w[:], ln2_w.rearrange("(p a) -> p a", a=1)),
                             (ln2b[:], ln2_b.rearrange("(p a) -> p a", a=1)),
                             (router[:], router_t),
                             (w1_sb[:], w1.rearrange("e h f -> h e f")),
                             (w2_sb[:], w2.rearrange("e (c f) h -> f e c h", c=FC))):
                with nc.allow_non_contiguous_dma(reason="the biases, once"):
                    sp.dma_start(dst, src).then_inc(s_dma_w2, 16)
            run_steps(sp, step)
            for p in range(2):
                sp.wait_ge(s_zd[p], 16 * NB // 2)

            load_z_group(0, 0)

            def group_step(g, p):
                ffn, tail, head, norm = group_present(g)
                if norm:
                    load_x_group(g + 3, 1 - p)
                if head:
                    load_z_group(g + 2, p)
                if ffn:
                    sp.wait_ge(s_acc, NE * (g + 1))
                    for q in range(QUAD):
                        sp.dma_start(rows(out, g, q), acc[p][q * SEQ:(q + 1) * SEQ]).then_inc(s_out[p], 16)

            run_groups(sp, group_step)
            for p in range(2):
                sp.wait_ge(s_out[p], 64 * GROUPS // 2)


_INS = ['L0_attn_x', 'L0_attn_Wq', 'L0_attn_Wk', 'L0_attn_Wv', 'L0_attn_Wo', 'L0_ffn_ln1_w', 'L0_ffn_ln1_b',
        'L0_ffn_in_proj_w', 'L0_ffn_in_proj_b', 'L0_ffn_out_proj_w', 'L0_ffn_out_proj_b', 'L0_ffn_ln2_w',
        'L0_ffn_ln2_b', 'L0_ffn_router_w', 'L0_ffn_w1', 'L0_ffn_w2']
_TRANSPOSED = ('L0_ffn_in_proj_w', 'L0_ffn_out_proj_w', 'L0_ffn_router_w')


def kernel(**inputs):
    import numpy as _np
    import concourse.bacc as _bacc
    from concourse import mybir as _mybir
    from concourse.bass_utils import run_bass_kernel_spmd as _run

    nc = _bacc.Bacc("TRN2", target_bir_lowering=False, num_devices=1)
    arrays, args = {}, []
    for name in _INS:
        a = _np.asarray(inputs[name])
        a = _np.ascontiguousarray(a.T if name in _TRANSPOSED else a)
        arrays[f"in_{name}"] = a
        args.append(nc.dram_tensor(f"in_{name}", a.shape, _mybir.dt.from_np(a.dtype), kind="ExternalInput").ap())
    out = nc.dram_tensor("out_0", (NB, NS, E), F32, kind="ExternalOutput").ap()
    attention_and_experts_kernel(nc, *args, out)
    r = _run(nc, [arrays], core_ids=[0])
    return r.results[0]["out_0"]
```
